# Optimizing a Trainium2 kernel written in Bass

```python
import numpy as np
import jax
import jax.numpy as jnp

def _softmax(x, axis=-1):
    return jax.nn.softmax(x, axis=axis)

def _gelu(x):
    return jax.nn.gelu(x, approximate=True)

def _silu(x):
    return jax.nn.silu(x)

def _sigmoid(x):
    return jax.nn.sigmoid(x)

def _layernorm(x, axis=-1, eps=1e-05):
    m = jnp.mean(x, axis=axis, keepdims=True)
    v = jnp.var(x, axis=axis, keepdims=True)
    return (x - m) / jnp.sqrt(v + eps)

def _scatter_add(tgt, idx, src, axis=0):
    return tgt.at[idx].add(src)

def _segment_sum(src, seg, n):
    return jax.ops.segment_sum(src, seg, n)
kernel_name = 'mk_xattn_ffn_d1_seqx_r8_5d8995'

def setup_inputs(seed: int=0):
    np.random.seed(seed)
    _w = jnp.asarray

    def _rec_inputs():
        import jax
        import jax.numpy as jnp
        _rk = jax.random.key(seed)
        x = -0.0005207 + 1.001 * jax.random.normal(jax.random.fold_in(_rk, 1), (64, 64, 128), jnp.float32)
        _lenS = 64 - jax.random.randint(jax.random.fold_in(_rk, 7), (64,), 0, max(1, 64 // 4) + 1, jnp.int32)
        _lenS2 = 64 - jax.random.randint(jax.random.fold_in(_rk, 8), (64,), 0, max(1, 64 // 4) + 1, jnp.int32)
        _ctx_1024P = jax.random.normal(jax.random.fold_in(_rk, 11), (64, 16, 128), jnp.float32)
        _ctx_1024c = jax.random.dirichlet(jax.random.fold_in(_rk, 511), 0.3 * jnp.ones((16,), jnp.float32), (64, 64))
        _ctx_1024t = jnp.einsum('bsk,bkd->bsd', _ctx_1024c, _ctx_1024P)
        _ctx_1024t = _ctx_1024t * jax.lax.rsqrt(jnp.mean(jnp.square(_ctx_1024t)) + 1e-12) * 0.953939
        ctx_1024 = -0.000514642 + 1.00011 * (_ctx_1024t + 0.3 * jax.random.normal(jax.random.fold_in(_rk, 611), (64, 64, 128), jnp.float32))
        _validS = jnp.arange(64)[None, :] < _lenS[:, None]
        _validS2 = jnp.arange(64)[None, :] < _lenS2[:, None]
        _causal = jnp.tril(jnp.ones((64, 64), dtype=bool))
        mask_1xSxS2_bf1 = jnp.ones((1, 64, 64), dtype=bool)
        return (x, ctx_1024, mask_1xSxS2_bf1)
    x, ctx_1024, mask_1xSxS2_bf1 = _rec_inputs()

    def _L0_xattn_setup():
        import jax, jax.numpy as jnp
        import numpy as np
        import math
        H_SIZE = 128
        N_HEADS = 16
        D_K = H_SIZE // N_HEADS

        def sinusoidal_pe(d_model, max_length):
            pos = jnp.arange(max_length, dtype=jnp.float32)[:, None]
            theta = pos / 10000.0 ** (jnp.arange(0, d_model, 2, dtype=jnp.float32) / d_model)
            pe = jnp.stack([jnp.sin(theta), jnp.cos(theta)], axis=-1).reshape(max_length, d_model)
            return pe

        def left_shift(x):
            L = x.shape[-2]
            M = x.shape[-1] - L
            flat = x.reshape(x.shape[:-2] + (-1,))
            i = jnp.arange(L)[:, None]
            j = jnp.arange(M)[None, :]
            idx = 2 * L - 1 + i * (M + L - 1) + j
            out = flat[..., idx]
            keep = j - i <= M - L
            return jnp.where(keep, out, jnp.zeros((), dtype=x.dtype))
        key = jax.random.key(seed)
        ks = jax.random.split(key, 12)
        B, T, S = (1, 256, 256)
        s = 1.0 / math.sqrt(H_SIZE)
        inp = {'q': jax.random.normal(ks[0], (B, T, H_SIZE), jnp.float32), 'k': jax.random.normal(ks[1], (B, S, H_SIZE), jnp.float32), 'v': jax.random.normal(ks[2], (B, S, H_SIZE), jnp.float32), 'mask': jnp.ones((B, T, S), dtype=bool), 'w_q': jax.random.normal(ks[3], (H_SIZE, H_SIZE), jnp.float32) * s, 'w_k': jax.random.normal(ks[4], (H_SIZE, H_SIZE), jnp.float32) * s, 'w_v': jax.random.normal(ks[5], (H_SIZE, H_SIZE), jnp.float32) * s, 'w_p': jax.random.normal(ks[6], (H_SIZE, H_SIZE), jnp.float32) * s, 'w_o': jax.random.normal(ks[7], (H_SIZE, H_SIZE), jnp.float32) * s, 'b_u': jax.random.uniform(ks[8], (N_HEADS, D_K), jnp.float32, -s, s), 'b_v': jax.random.uniform(ks[9], (N_HEADS, D_K), jnp.float32, -s, s)}
        return inp
    _L0_xattn_all = _L0_xattn_setup()
    _L0_xattn_in = {k: v for k, v in _L0_xattn_all.items() if k in ('w_q', 'w_k', 'w_v', 'w_p', 'w_o', 'b_u', 'b_v')}
    del _L0_xattn_all

    def _L0_ffn_setup():
        import jax, jax.numpy as jnp
        import numpy as np
        H = 128
        I = 128
        E = 8
        key = jax.random.key(seed)
        ks = jax.random.split(key, 8)
        s = 0.02
        x = jax.random.normal(ks[0], (4, 256, H), dtype=jnp.float32)
        Wg = jax.random.normal(ks[1], (H, E), dtype=jnp.float32) * s
        bg = jnp.zeros((E,), dtype=jnp.float32)
        W1 = jax.random.normal(ks[2], (E, H, I), dtype=jnp.float32) * s
        b1 = jnp.zeros((E, I), dtype=jnp.float32)
        W2 = jax.random.normal(ks[3], (E, I, H), dtype=jnp.float32) * s
        b2 = jnp.zeros((E, H), dtype=jnp.float32)
        return {'x': x, 'Wg': Wg, 'bg': bg, 'W1': W1, 'b1': b1, 'W2': W2, 'b2': b2}
    _L0_ffn_all = _L0_ffn_setup()
    _L0_ffn_in = {k: v for k, v in _L0_ffn_all.items() if k in ('Wg', 'bg', 'W1', 'b1', 'W2', 'b2')}
    del _L0_ffn_all
    return {'x': x, 'ctx_1024': ctx_1024, 'mask_1xSxS2_bf1': mask_1xSxS2_bf1, 'L0_xattn_w_q': _L0_xattn_in['w_q'], 'L0_xattn_w_k': _L0_xattn_in['w_k'], 'L0_xattn_w_v': _L0_xattn_in['w_v'], 'L0_xattn_w_p': _L0_xattn_in['w_p'], 'L0_xattn_w_o': _L0_xattn_in['w_o'], 'L0_xattn_b_u': _L0_xattn_in['b_u'], 'L0_xattn_b_v': _L0_xattn_in['b_v'], 'L0_ffn_Wg': _L0_ffn_in['Wg'], 'L0_ffn_bg': _L0_ffn_in['bg'], 'L0_ffn_W1': _L0_ffn_in['W1'], 'L0_ffn_b1': _L0_ffn_in['b1'], 'L0_ffn_W2': _L0_ffn_in['W2'], 'L0_ffn_b2': _L0_ffn_in['b2']}

def reference(x, ctx_1024, mask_1xSxS2_bf1, L0_xattn_w_q, L0_xattn_w_k, L0_xattn_w_v, L0_xattn_w_p, L0_xattn_w_o, L0_xattn_b_u, L0_xattn_b_v, L0_ffn_Wg, L0_ffn_bg, L0_ffn_W1, L0_ffn_b1, L0_ffn_W2, L0_ffn_b2):
    import jax
    import jax.numpy as jnp

    def _L0_xattn_ref(q, k, v, mask, w_q, w_k, w_v, w_p, w_o, b_u, b_v):
        import jax, jax.numpy as jnp
        import numpy as np
        import math
        H_SIZE = 128
        N_HEADS = 16
        D_K = H_SIZE // N_HEADS

        def sinusoidal_pe(d_model, max_length):
            pos = jnp.arange(max_length, dtype=jnp.float32)[:, None]
            theta = pos / 10000.0 ** (jnp.arange(0, d_model, 2, dtype=jnp.float32) / d_model)
            pe = jnp.stack([jnp.sin(theta), jnp.cos(theta)], axis=-1).reshape(max_length, d_model)
            return pe

        def left_shift(x):
            L = x.shape[-2]
            M = x.shape[-1] - L
            flat = x.reshape(x.shape[:-2] + (-1,))
            i = jnp.arange(L)[:, None]
            j = jnp.arange(M)[None, :]
            idx = 2 * L - 1 + i * (M + L - 1) + j
            out = flat[..., idx]
            keep = j - i <= M - L
            return jnp.where(keep, out, jnp.zeros((), dtype=x.dtype))
        b, t, _ = q.shape
        s = k.shape[1]
        qh = (q @ w_q).reshape(b, t, N_HEADS, D_K).transpose(0, 2, 1, 3)
        kh = (k @ w_k).reshape(b, s, N_HEADS, D_K).transpose(0, 2, 1, 3)
        vh = (v @ w_v).reshape(b, s, N_HEADS, D_K).transpose(0, 2, 1, 3)
        pe = sinusoidal_pe(H_SIZE, 2 * s)[::-1].astype(q.dtype)
        ph = (pe @ w_p).reshape(2 * s, N_HEADS, D_K).transpose(1, 0, 2)
        ac = jnp.einsum('bhtd,bhsd->bhts', qh + b_u[None, :, None, :], kh)
        bd = jnp.einsum('bhtd,hmd->bhtm', qh + b_v[None, :, None, :], ph)
        bd = left_shift(bd)
        scores = (ac + bd) / math.sqrt(D_K)
        scores = jnp.where(mask[:, None, :, :], scores, jnp.float32(-jnp.inf))
        attn = jax.nn.softmax(scores, axis=-1)
        out = jnp.einsum('bhts,bhsd->bthd', attn, vh).reshape(b, t, H_SIZE)
        return out @ w_o

    def _L0_ffn_ref(x, Wg, bg, W1, b1, W2, b2):
        import jax, jax.numpy as jnp
        import numpy as np
        H = 128
        I = 128
        E = 8
        B, S, Hd = x.shape
        xf = x.reshape(-1, Hd)
        logits = xf @ Wg + bg
        gates = jax.nn.softmax(logits, axis=-1)
        idx = jnp.argmax(gates, axis=-1)
        h = jax.nn.gelu(jnp.einsum('th,ehi->tei', xf, W1) + b1, approximate=False)
        y = jnp.einsum('tei,eih->teh', h, W2) + b2
        out = jnp.take_along_axis(y, idx[:, None, None], axis=1)[:, 0, :]
        return out.reshape(B, S, Hd)
    x = x + _L0_xattn_ref(_layernorm(x, axis=-1), ctx_1024, ctx_1024, mask_1xSxS2_bf1, L0_xattn_w_q, L0_xattn_w_k, L0_xattn_w_v, L0_xattn_w_p, L0_xattn_w_o, L0_xattn_b_u, L0_xattn_b_v)
    x = x + _L0_ffn_ref(_layernorm(x, axis=-1), L0_ffn_Wg, L0_ffn_bg, L0_ffn_W1, L0_ffn_b1, L0_ffn_W2, L0_ffn_b2)
    return x

_drawn_inputs = setup_inputs


def setup_inputs(seed=0):
    import zlib

    import numpy as np

    out = dict(_drawn_inputs(seed))
    spreads = {'L0_ffn_bg': (0.0, 0.1), 'L0_ffn_b1': (0.0, 0.8), 'L0_ffn_b2': (0.0, 0.1)}
    factors = {'L0_xattn_b_u': 3.86, 'L0_xattn_b_v': 8.0}
    for name, (base, spread) in spreads.items():
        noise = np.random.default_rng([zlib.crc32(name.encode()), seed]).standard_normal(out[name].shape)
        drawn = base * np.exp(spread * noise) if base else spread * noise
        out[name] = jnp.asarray(drawn.astype(out[name].dtype))
    for name, factor in factors.items():
        out[name] = (out[name] * factor).astype(out[name].dtype)
    return out
```

```python
from contextlib import ExitStack

import concourse.bass as bass
from concourse import mybir

F32 = mybir.dt.float32
BF16 = mybir.dt.bfloat16
U8 = mybir.dt.uint8
ALU = mybir.AluOpType
ACT = mybir.ActivationFunctionType
AX = mybir.AxisListType.X

B, T, D = 64, 64, 128
H, DK = 16, 8
HP = H // 2
E = 8
GB = 16
G = B // GB
GT = GB * T
HT = GT // 2
TT = HT // 128
NT = GT // 128
IH = 16
NM = H // 4
NQ = G * NM
NU = 2 * NQ
EPS = 1e-5
SCALE = float(DK) ** -0.5
NEG = 1e30
Q_PART = (0, 0, 0, 1, 1, 2)
K_PART = (0, 1, 2, 0, 1, 0)
NS = len(Q_PART)
KC = NS * 2 * DK
KB = KC + 6
VW = DK + 1


def schedule():
    def front(k):
        items = []
        for hf in range(2):
            items += [(0, ("load", k, hf)), (0, ("ln1", k, hf)), (9, ("xT", k, hf)), (9, ("cT", k, hf)), (9, ("q", k, hf)),
                      (9, ("k", k, hf)), (14, ("v", k, hf))]
        return items + [(0, ("stack", k))]

    def post(k):
        items = [(0, ("norm", k, hf)) for hf in range(2)]
        for hf in range(2):
            items += [(0, ("load_x1", k, hf)), (9, ("aT", k, hf)), (14, ("proj", k, hf)), (0, ("ln2", k, hf)),
                      (9, ("x2T", k, hf)), (5, ("gate", k, hf)), (5, ("ohT", k, hf)),
                      (2, ("sel", k, hf, 0)), (2, ("sel", k, hf, 1))]
            for e in range(E):
                if e + 2 < E:
                    items.append((2, ("sel", k, hf, e + 2)))
                items.append((9, ("up", k, hf, e)))
            items.append((2, ("gelu", k, hf)))
            items += [(9, ("down", k, hf, e)) for e in range(E)]
            items += [(2, ("y", k, hf)), (9, ("out", k, hf))]
        return items

    def merged(a, b):
        out = []
        for items in (a, b):
            total, at = sum(c for c, _ in items) or 1, 0
            for c, item in items:
                out.append(((at + 0.5 * c) / total, c, item))
                at += c
        return [(c, item) for _, c, item in sorted(out, key=lambda x: x[0])]

    out = [item for _, item in front(0)]
    for g in range(G + 1):
        ahead = front(g + 1) if g + 1 < G else []
        behind = post(g - 1) if g else []
        if g == G:
            out.append(("pv", NQ - 1))
            out += [item for _, item in behind]
            break
        fill = merged(ahead, behind)
        total, at, done = sum(c for c, _ in fill), 0, 0
        slots = 6 * NM - 3
        for hp in range(2 * NM):
            u = 2 * NM * g + hp
            for s, own in enumerate((("scores", u), ("rows", u), ("shift", u))):
                if own[0] == "shift":
                    if u and u % 2 == 0:
                        out.append(("pv", u // 2 - 1))
                out.append(own)
                if hp == 0:
                    continue
                done += 1
                while fill and at < total * done / slots:
                    c, item = fill.pop(0)
                    out.append(item)
                    at += c
        out += [item for _, item in fill]
    return out


MISC = ("xT", "cT", "q", "k", "v", "aT", "proj", "x2T", "gate", "ohT", "sel", "out")


def xattn_moe_kernel(nc, x, ctx_in, mask, w_q, w_k, w_v, w_p, w_o, b_u, b_v, Wg, bg, W1, b1, W2, b2,
                     c_ident, c_pe, c_small, c_shift, c_ones, out):
    steps = schedule()
    turn = {item: n + 2 for n, item in enumerate(i for i in steps if i[0] in MISC)}

    x_t = x.rearrange("(k b) t d -> k (b t) d", b=GB).rearrange("k (c n p) d -> (k c) p n d", c=2, p=128)
    c_t = ctx_in.rearrange("(k b) t d -> k (b t) d", b=GB).rearrange("k (c n p) d -> (k c) p n d", c=2, p=128)
    o_t = out.rearrange("(k b) t d -> k (b t) d", b=GB).rearrange("k (c n p) d -> (k c) p n d", c=2, p=128)
    q_dram = nc.dram_tensor("q_parts", (G, 3, D, GT), BF16, kind="Internal").ap()
    k_dram = nc.dram_tensor("k_parts", (G, 3, D, GT), BF16, kind="Internal").ap()
    p_dram = nc.dram_tensor("p_parts", (3, D, 128), BF16, kind="Internal").ap()
    c_dram = nc.dram_tensor("c_parts", (3, H, 128), BF16, kind="Internal").ap()

    ctx = ExitStack()
    with ctx:
        def sb(name, shape, dt=F32):
            return ctx.enter_context(nc.sbuf_tensor(name, shape, dt))

        def sem(name):
            return ctx.enter_context(nc.semaphore(name))

        ident = sb("ident", [128, 128])
        pe_rev = sb("pe_rev", [128, 128])
        small = sb("small", [128, 64])
        head_of = small[:, 0:16]
        minus_lo = small[:, 16:17]
        shift_own = small[:, 17:49]
        order = small[:, 49:57]
        shift_f = sb("shift_f", [128, 128])
        wq, wk, wv, wp, wo = (sb(n, [128, 128]) for n in ("wq", "wk", "wv", "wp", "wo"))
        w1 = sb("w1", [128, E, 128])
        w2 = sb("w2", [128, E, 128])
        wg = sb("wg", [128, E])
        bg_row = sb("bg_row", [128, E])
        bu = sb("bu", [128, 1])
        bv = sb("bv", [128, 1])
        b12 = sb("b12", [E, 2, 128])
        mask_u = sb("mask_u", [128, 64], U8)
        mask_f = sb("mask_f", [128, 64])
        mask_neg = sb("mask_neg", [64, 2, 64], BF16)
        ident_h = sb("ident_h", [128, 128], BF16)
        shift_sel = sb("shift_sel", [128, 128], BF16)
        bias_diff = sb("bias_diff", [128, 1])
        bias_heads = sb("bias_heads", [128, H])
        any_key = sb("any_key", [128, 4])
        rev = sb("rev", [128, 2, 128])
        rev_part = sb("rev_part", [128, 3, 128], BF16)
        cst = sb("cst", [H, 2, 128])
        cst_part = sb("cst_part", [H, 3, 128], BF16)
        b12_rest = sb("b12_rest", [E, 2, 128])
        b12_part = sb("b12_part", [E, 2, 3, 128], BF16)
        b12_rows = sb("b12_rows", [3 * E, 2, 128], BF16)
        pos = sb("pos", [128, HP, 128], BF16)
        x_in = sb("x_in", [128, TT, D])
        c_in = sb("c_in", [128, TT, D])
        stats = sb("stats", [128, TT, 6])
        mv = sb("mv", [128, TT, 2])
        vare = sb("vare", [128, TT])
        rstd = sb("rstd", [128, TT])
        mhalf = sb("mhalf", [128, TT])
        xn = sb("xn", [128, TT, D])
        xT = sb("xT", [128, HT])
        cT = sb("cT", [128, HT])
        qf = sb("qf", [128, HT])
        kf = sb("kf", [128, HT])
        r1q = sb("r1q", [128, HT])
        r1k = sb("r1k", [128, HT])
        r1_of = {"q": r1q, "k": r1k}
        q_part = sb("q_part", [128, 3, GT], BF16)
        k_part = sb("k_part", [128, 3, GT], BF16)
        q_st = [sb(f"q_st{i}", [128, HP // 2, 2, GT], BF16) for i in range(3)]
        k_st = [sb(f"k_st{i}", [128, HP // 2, GT], BF16) for i in range(3)]
        val = [sb(f"val{i}", [128, GB, HP, 2 * VW]) for i in range(2)]
        colmax = sb("colmax", [128, 2, 32])
        rowmax = sb("rowmax", [128, 32])
        rowmax_h = sb("rowmax_h", [128, 32], BF16)
        shift_v = sb("shift_v", [128, 2, 32], BF16)
        shift_x = sb("shift_x", [128, 2, 2, 16, 32], BF16)
        prob = sb("prob", [128, 2, 2 * GB, T])
        att = sb("att", [128, NT, HP, 2 * VW])
        rden = sb("rden", [128, TT * H])
        att_n = sb("att_n", [128, 2, TT, D])
        x_res = sb("x_res", [128, TT, D])
        aT = sb("aT", [128, HT])
        x1 = sb("x1", [128, 2, TT, D])
        stats2 = sb("stats2", [128, TT, 6])
        mv2 = sb("mv2", [128, TT, 2])
        vare2 = sb("vare2", [128, TT])
        rstd2 = sb("rstd2", [128, TT])
        xn2 = sb("xn2", [128, TT, D])
        x2T = sb("x2T", [128, HT])
        logit = sb("logit", [128, TT, E])
        top = sb("top", [128, TT])
        first = sb("first", [128, TT])
        is_top = sb("is_top", [128, TT, E])
        key = sb("key", [128, TT, E])
        onehot = sb("onehot", [128, TT, 3, E])
        ohT = sb("ohT", [3 * E, HT], BF16)
        chosen = sb("chosen", [128, E, HT], BF16)
        picked = sb("picked", [128, 4, HT])
        hid = sb("hid", [128, HT])
        yT = sb("yT", [128, HT])

        ps = ctx.enter_context(nc.psum_tensor("ps", [128, 8, 512], F32))
        score = [[ps[:, 2 * p + ih, :] for ih in range(2)] for p in range(2)]
        row_ps = ps[:, 4, 0:64]
        pv_ps = ps[:, 4, 64:64 + NT * 4 * VW]
        ffn_ps = ps[:, 5, :]
        misc = [ps[:, 6, :], ps[:, 7, :]]

        names = """ones consts masks_loaded zeroed prep ph_rev ph_cst rev_split cst_split bias_split p_out c_out pos_in bias_in
            x_in c_in stats mv vare rstd xn xT cT cT_used qf qh r1q qm ql kf kh r1k km kl q_out k_out q_in0 q_in1 q_in2 k_in0 k_in1 k_in2 v_in
            scored colmaxed rows rowmaxed rowmax_h shift_v shift_x shifted prob pv att
            rden attn_n aT x_res x1 stats2 mv2 vare2 rstd2 xn2 x2T logit top is_top key first onehot ohT
            chosen picked_v picked_p up down hid yT y_out stored0 stored1 full0 full1 free0 free1 ffn_full ffn_free proj_done
            xT_used q_done k_done gated hid_used yT_used aT_used""".split()
        S = {n: sem("s_" + n) for n in names}
        full = [S["full0"], S["full1"]]
        free = [S["free0"], S["free1"]]
        q_in = [S[f"q_in{i}"] for i in range(3)]
        k_in = [S[f"k_in{i}"] for i in range(3)]
        stored = [S["stored0"], S["stored1"]]
        N_CONST = 20 - 1

        def fill_wait(eng, item):
            n = turn[item] if isinstance(item, tuple) else item
            if n >= 2:
                eng.wait_ge(free[n % 2], n // 2)
            return misc[n % 2], full[n % 2]

        def read_wait(eng, item):
            n = turn[item] if isinstance(item, tuple) else item
            eng.wait_ge(full[n % 2], n // 2 + 1)
            return misc[n % 2], free[n % 2]

        def pick(eng, done, what, c, e, n):
            eng.wait_ge(S["chosen"], E * c + e + 1)
            if what == "up":
                eng.wait_ge(S["x2T"], c + 1)
                src = x2T
            else:
                eng.wait_ge(S["hid"], c + 1)
                src = hid
            if n >= 2:
                m = n - 2
                half, kind, i = m // E, (m // (E // 2)) % 2, m % (E // 2)
                eng.wait_ge(S[("up", "down")[kind]], E * half + 2 * i + e % 2 + 1)
            eng.tensor_tensor(picked[:, 2 * (e % 2) + n % 2, :], src[:], chosen[:, e, :], ALU.mult).then_inc(done, 1)

        block = ctx.enter_context(nc.Block())

        @block.sync
        def _(sp):
            for dst, src in ((ident[:], c_ident), (pe_rev[:], c_pe), (small[:], c_small), (shift_f[:], c_shift),
                             (wp[:], w_p), (wq[:], w_q), (wk[:], w_k), (wv[:], w_v), (wo[:], w_o),
                             (bu[:], b_u.rearrange("h (d one) -> (h d) one", one=1)),
                             (bv[:], b_v.rearrange("h (d one) -> (h d) one", one=1)),
                             (wg[:], Wg), (bg_row[:], bg.partition_broadcast(128)),
                             (b12[:, 0, :], b1), (b12[:, 1, :], b2),
                             (w1[:], W1.rearrange("e d i -> d e i")), (w2[:], W2.rearrange("e i d -> i e d")),
                             (mask_u[0:64, :], mask[0]), (mask_u[64:128, :], mask[0])):
                sp.dma_start(dst, src).then_inc(S["consts"], 16)

            for i in range(3):
                sp.dma_start(q_st[i][KC:KB, :, :, :], c_ones.bitcast(BF16)).then_inc(S["ones"], 16)

            for item in steps:
                what, k = item[0], item[1]
                if what == "load":
                    c = 2 * k + item[2]
                    if c:
                        sp.wait_ge(S["xn"], c * TT)
                    sp.dma_start(x_in[:], x_t[c]).then_inc(S["x_in"], 16)
                    if c:
                        sp.wait_ge(S["cT"], c)
                    sp.dma_start(c_in[:], c_t[c]).then_inc(S["c_in"], 16)
                    if c == 0:
                        sp.wait_ge(S["rev_split"], 4)
                        sp.dma_start(p_dram.rearrange("s p t -> p s t"), rev_part[:]).then_inc(S["p_out"], 16)
                        sp.wait_ge(S["cst_split"], 4)
                        sp.dma_start(c_dram.rearrange("s h t -> h s t"), cst_part[:]).then_inc(S["c_out"], 16)
                        sp.wait_ge(S["bias_split"], 4)
                        for s in range(3):
                            sp.dma_start(b12_rows[s * E:(s + 1) * E, :, :], b12_part[:, :, s, :])\
                              .then_inc(S["bias_in"], 16)
                        sp.wait_ge(S["p_out"], 16)
                        sp.wait_ge(S["zeroed"], 6)
                        for s in range(NS):
                            src = p_dram[K_PART[s]].rearrange("(hp r) t -> r hp t", r=2 * DK)
                            sp.dma_start(pos[s * 2 * DK:(s + 1) * 2 * DK, :, :], src).then_inc(S["pos_in"], 16)
                        sp.wait_ge(S["c_out"], 16)
                        for s in range(3):
                            src = c_dram[s].rearrange("(hp h2) t -> h2 hp t", h2=2)
                            sp.dma_start(pos[KC + 2 * s:KC + 2 * s + 2, :, :], src).then_inc(S["pos_in"], 16)
                elif what == "stack":
                    sp.wait_ge(S["qh"], 2 * k + 2)
                    sp.wait_ge(S["qm"], 2 * k + 2)
                    sp.wait_ge(S["ql"], 2 * k + 2)
                    sp.dma_start(q_dram[k].rearrange("s p t -> p s t"), q_part[:]).then_inc(S["q_out"], 16)
                    sp.wait_ge(S["kh"], 2 * k + 2)
                    sp.wait_ge(S["km"], 2 * k + 2)
                    sp.wait_ge(S["kl"], 2 * k + 2)
                    sp.dma_start(k_dram[k].rearrange("s p t -> p s t"), k_part[:]).then_inc(S["k_out"], 16)
                    sp.wait_ge(S["q_out"], 16 * (k + 1))
                    sp.wait_ge(S["k_out"], 16 * (k + 1))
                    if k == 0:
                        sp.wait_ge(S["zeroed"], 6)
                    for m in range(2):
                        n = 2 * k + m
                        if n >= 3:
                            sp.wait_ge(S["scored"], 2 * NM * (n - 2))
                        for s in range(NS):
                            src = k_dram[k, K_PART[s]].rearrange("(hpar mh ml r) t -> mh hpar r ml t", hpar=2, mh=2, ml=2)
                            for hpar in range(2):
                                sp.dma_start(k_st[n % 3][s * 2 * DK:(s + 1) * 2 * DK, 2 * hpar:2 * hpar + 2, :],
                                             src[m, hpar]).then_inc(k_in[n % 3], 16)
                            src = q_dram[k, Q_PART[s]].rearrange("(hpar mh ml h2 d) t -> mh h2 hpar d ml t",
                                                                 hpar=2, mh=2, ml=2, h2=2)
                            for h2 in range(2):
                                r = (s * 2 + h2) * DK
                                for hpar in range(2):
                                    sp.dma_start(q_st[n % 3][r:r + DK, 2 * hpar:2 * hpar + 2, h2, :],
                                                 src[m, h2, hpar]).then_inc(q_in[n % 3], 16)
                elif what == "load_x1":
                    c = 2 * k + item[2]
                    if c:
                        sp.wait_ge(S["x1"], c)
                    sp.dma_start(x_res[:], x_t[c]).then_inc(S["x_res"], 16)
                elif what == "out":
                    hf = item[2]
                    sp.wait_ge(S["y_out"], 2 * k + hf + 1)
                    sp.dma_start(o_t[2 * k + hf], x1[:, hf, :, :]).then_inc(stored[hf], 16)
            for hf in range(2):
                sp.wait_ge(stored[hf], 16 * G)

        @block.gpsimd
        def _(pool):
            pool.memset(pos[:], 0.0).then_inc(S["zeroed"], 1)
            pool.memset(mhalf[:], -0.5).then_inc(S["zeroed"], 1)
            for i in range(3):
                pool.memset(q_st[i][0:KC, :, :, :], 0.0).then_inc(S["zeroed"], 1)
            pool.memset(colmax[:], 0.0).then_inc(S["zeroed"], 1)

            def inverse_root(c, stat, variance, scaled, root, suffix):
                pool.wait_ge(S["mv" + suffix], TT * (c + 1))
                if c:
                    pool.wait_ge(S["rstd" + suffix], c)
                    pool.wait_ge(S["xn" + suffix], TT * c)
                pool.tensor_scalar(scaled[:], variance, EPS, None, ALU.add).then_inc(S["vare" + suffix], 1)
                pool.wait_ge(S["vare" + suffix], c + 1)
                pool.tensor_tensor(root[:], scaled[:], mhalf[:], ALU.pow).then_inc(S["rstd" + suffix], 1)

            for item in steps:
                what, k = item[0], item[1]
                c = 2 * k + item[2] if len(item) > 2 else None
                if what == "ln1":
                    inverse_root(c, stats, mv[:, :, 1], vare, rstd, "")
                elif what == "ln2":
                    inverse_root(c, stats2, mv2[:, :, 1], vare2, rstd2, "2")
                elif what in ("q", "k"):
                    hf = item[2]
                    part = q_part if what == "q" else k_part
                    rest = r1_of[what]
                    pool.wait_ge(S[what + "m"], c + 1)
                    if k and hf == 0:
                        pool.wait_ge(S[what + "_out"], 16 * k)
                    pool.tensor_tensor(part[:, 2, hf * HT:(hf + 1) * HT], rest[:], part[:, 1, hf * HT:(hf + 1) * HT],
                                       ALU.subtract).then_inc(S[what + "l"], 1)
                elif what == "shift":
                    u = k
                    pool.wait_ge(S["shift_v"], u + 1)
                    if u >= 2:
                        pool.wait_ge(S["shifted"], u - 1)
                    for iq in range(2):
                        own = shift_own[:, iq * 16:(iq + 1) * 16]
                        pool.tensor_tensor(shift_x[:, u % 2, iq, :, :],
                                           shift_v[:, u % 2, :].unsqueeze(1).broadcast_to([128, 16, 32]),
                                           own.unsqueeze(2).broadcast_to([128, 16, 32]), ALU.mult)\
                            .then_inc(S["shift_x"], 1)
                elif what in ("up", "down") and item[3] % 2:
                    c, e = 2 * k + item[2], item[3]
                    n = (E // 2) * (2 * c + (what == "down")) + e // 2
                    pick(pool, S["picked_p"], what, c, e, n)


        @block.scalar
        def _(act):
            for item in steps:
                what, k = item[0], item[1]
                if what == "shift":
                    u = k
                    act.wait_ge(S["shifted"], u + 1)
                    v, ih = divmod(u, 2)
                    if v >= 2:
                        act.wait_ge(S["pv"], v - 1)
                    for iq in range(2):
                        i = (2 * ih + iq) * IH
                        act.activation(prob[:, v % 2, :, i:i + IH], score[u % 2][iq].rearrange(
                            "p (hb i) -> p hb i", i=IH), ACT.Exp, scale=SCALE).then_inc(S["prob"], 1)
                    continue
                if what == "pv":
                    act.wait_ge(S["pv"], k + 1)
                    g, m = divmod(k, NM)
                    if m == 0 and g:
                        act.wait_ge(S["attn_n"], 4 * g)
                    act.activation(att[:, :, 2 * m:2 * m + 2, :].rearrange("p n h v -> p n (h v)"),
                                   pv_ps.rearrange("p (n v) -> p n v", v=4 * VW), ACT.Copy)\
                       .then_inc(S["att"], 1)
                    continue
                if len(item) < 3 or what in ("load", "load_x1"):
                    continue
                hf = item[2]
                c = 2 * k + hf
                cols = slice(hf * HT, (hf + 1) * HT)
                if what in ("xT", "cT"):
                    bank, done = read_wait(act, item)
                    if c:
                        act.wait_ge(S["q_done" if what == "xT" else "cT_used"], c)
                    act.activation((xT if what == "xT" else cT)[:], bank, ACT.Copy).then_inc(S[what], 1)
                    act.wait_ge(S[what], c + 1)
                    act.sem_inc(done, 1)
                elif what in ("q", "k"):
                    bank, done = read_wait(act, item)
                    full_f, part = (qf, q_part) if what == "q" else (kf, k_part)
                    if c:
                        act.wait_ge(S["r1" + what], c)
                    func, args = (ACT.Identity, {"bias": bu[:, 0:1]}) if what == "q" else (ACT.Copy, {})
                    if what == "q" and c == 0:
                        act.wait_ge(S["consts"], 16 * N_CONST)
                    act.activation(full_f[:], bank, func, **args).then_inc(S[what + "f"], 1)
                    if k and hf == 0:
                        act.wait_ge(S[what + "_out"], 16 * k)
                    act.activation(part[:, 0, cols], bank, func, **args).then_inc(S[what + "h"], 1)
                    act.wait_ge(S[what + "h"], c + 1)
                    act.sem_inc(done, 1)
                elif what == "v" :
                    bank, done = read_wait(act, item)
                    if k >= 2:
                        act.wait_ge(S["pv"], NM * (k - 1))
                    if c < 4:
                        act.wait_ge(S["prep"], 1)
                    for bp in range(2):
                        for hpar in range(2):
                            dst = val[k % 2][64 * hpar:64 * hpar + 64, :, :, :].rearrange(
                                "p (n bp) h v -> p n bp h v", bp=2)[:, hf * TT:(hf + 1) * TT, bp, :,
                                                                    hpar * VW:hpar * VW + DK]
                            src = bank[64 * bp:64 * bp + 64, :].rearrange(
                                "p (n hpar h d) -> p n hpar h d", n=TT, hpar=2, d=DK)[:, :, hpar, :, :]
                            act.activation(dst, src, ACT.Copy).then_inc(S["v_in"], 1)
                    act.wait_ge(S["v_in"], 4 * (c + 1))
                    act.sem_inc(done, 1)
                elif what == "aT":
                    bank, done = read_wait(act, item)
                    if c:
                        act.wait_ge(S["proj_done"], c)
                    act.activation(aT[:], bank, ACT.Copy).then_inc(S["aT"], 1)
                    act.wait_ge(S["aT"], c + 1)
                    act.sem_inc(done, 1)
                elif what == "x2T":
                    bank, done = read_wait(act, item)
                    if c:
                        act.wait_ge(S["gated"], c)
                        act.wait_ge(S["picked_v"], E * (c - 1) + E // 2)
                        act.wait_ge(S["picked_p"], E * (c - 1) + E // 2)
                    act.activation(x2T[:], bank, ACT.Copy).then_inc(S["x2T"], 1)
                    act.wait_ge(S["x2T"], c + 1)
                    act.sem_inc(done, 1)
                elif what == "ohT":
                    bank, done = read_wait(act, item)
                    if c:
                        act.wait_ge(S["ffn_full"], 2 * c)
                    act.activation(ohT[:], bank[0:3 * E, :], ACT.Copy).then_inc(S["ohT"], 1)
                    act.wait_ge(S["ohT"], c + 1)
                    act.sem_inc(done, 1)
                elif what == "sel":
                    e = item[3]
                    bank, done = read_wait(act, item)
                    if c:
                        act.wait_ge(S["picked_p" if e % 2 else "picked_v"], E * (c - 1) + E // 2 + e // 2 + 1)
                    act.activation(chosen[:, e, :], bank, ACT.Copy).then_inc(S["chosen"], 1)
                    act.wait_ge(S["chosen"], E * c + e + 1)
                    act.sem_inc(done, 1)
                elif what == "gelu":
                    act.wait_ge(S["ffn_full"], 2 * c + 1)
                    if c:
                        act.wait_ge(S["picked_v"], E * c)
                        act.wait_ge(S["picked_p"], E * c)
                    act.activation(hid[:], ffn_ps, ACT.Gelu).then_inc(S["hid"], 1)
                elif what == "y":
                    act.wait_ge(S["ffn_full"], 2 * c + 2)
                    if c:
                        act.wait_ge(S["yT_used"], c)
                    act.activation(yT[:], ffn_ps, ACT.Copy).then_inc(S["yT"], 1)

        @block.vector
        def _(dve):
            for i in range(2):
                dve.memset(val[i][:], 0.0).then_inc(S["masks_loaded"], 1)
            dve.wait_ge(S["masks_loaded"], 2)
            for i in range(2):
                for h2 in range(2):
                    dve.memset(val[i][64 * h2:64 * h2 + 64, :, :, h2 * VW + DK], 1.0).then_inc(S["masks_loaded"], 1)
            dve.wait_ge(S["consts"], 16 * N_CONST)
            dve.tensor_copy(ident_h[:], ident[:]).then_inc(S["masks_loaded"], 1)
            dve.tensor_copy(shift_sel[:], shift_f[:]).then_inc(S["masks_loaded"], 1)
            dve.tensor_copy(mask_f[:], mask_u[:]).then_inc(S["masks_loaded"], 1)
            dve.tensor_tensor(bias_diff[:], bv[:], bu[:], ALU.subtract).then_inc(S["masks_loaded"], 1)
            dve.wait_ge(S["masks_loaded"], 10)
            dve.tensor_scalar(bias_heads[:], head_of, bias_diff[:, 0:1], None, ALU.mult).then_inc(S["masks_loaded"], 1)
            for h2 in range(2):
                dve.tensor_scalar(mask_neg[:, h2, :], mask_f[0:64, :], 1.0, NEG, ALU.subtract, ALU.mult)\
                   .then_inc(S["masks_loaded"], 1)
            dve.tensor_reduce(any_key[:, 0:1], mask_f[:], AX, ALU.max).then_inc(S["masks_loaded"], 1)
            dve.wait_ge(S["masks_loaded"], 14)
            dve.reciprocal(any_key[:, 1:2], any_key[:, 0:1]).then_inc(S["masks_loaded"], 1)
            dve.wait_ge(S["masks_loaded"], 15)
            dve.tensor_tensor(any_key[:, 2:3], any_key[:, 0:1], any_key[:, 1:2], ALU.mult).then_inc(S["prep"], 1)

            def split(whole, rest, parts, done, n):
                dve.tensor_copy(parts[0], whole).then_inc(done, 1)
                dve.wait_ge(done, n + 1)
                dve.tensor_tensor(rest, whole, parts[0], ALU.subtract).then_inc(done, 1)
                dve.wait_ge(done, n + 2)
                dve.tensor_copy(parts[1], rest).then_inc(done, 1)
                dve.wait_ge(done, n + 3)
                dve.tensor_tensor(parts[2], rest, parts[1], ALU.subtract).then_inc(done, 1)

            bank, done = read_wait(dve, 0)
            dve.tensor_copy(rev[:, 0, :], bank[:, 0:128]).then_inc(S["ph_rev"], 1)
            dve.wait_ge(S["ph_rev"], 1)
            dve.sem_inc(done, 1)
            split(rev[:, 0, :], rev[:, 1, :], [rev_part[:, s, :] for s in range(3)], S["rev_split"], 0)
            bank, done = read_wait(dve, 1)
            dve.tensor_copy(cst[:, 0, :], bank[0:H, 0:128]).then_inc(S["ph_cst"], 1)
            dve.wait_ge(S["ph_cst"], 1)
            dve.sem_inc(done, 1)
            split(cst[:, 0, :], cst[:, 1, :], [cst_part[:, s, :] for s in range(3)], S["cst_split"], 0)
            split(b12[:], b12_rest[:], [b12_part[:, :, s, :] for s in range(3)], S["bias_split"], 0)

            def norm_stats(c, tiles, stat, agg, suffix):
                if c:
                    dve.wait_ge(S["xn" + suffix], TT * c)
                    dve.wait_ge(S["rstd" + suffix], c)
                for t in range(TT):
                    dve.bn_stats(stat[:, t, :], tiles(t)).then_inc(S["stats" + suffix], 1)
                for t in range(TT):
                    dve.wait_ge(S["stats" + suffix], TT * c + t + 1)
                    dve.bn_aggr(agg[:, t, :], stat[:, t, :]).then_inc(S["mv" + suffix], 1)

            def norm_apply(c, tiles, agg, root, dst, suffix):
                dve.wait_ge(S["rstd" + suffix], c + 1)
                dve.wait_ge(S["mv" + suffix], TT * (c + 1))
                for t in range(TT):
                    dve.tensor_scalar(dst[:, t, :], tiles(t), agg[:, t, 0:1], root[:, t:t + 1],
                                      ALU.subtract, ALU.mult).then_inc(S["xn" + suffix], 1)

            for item in steps:
                what, k = item[0], item[1]
                if what == "scores":
                    u = k
                    if u == 0:
                        dve.wait_ge(S["zeroed"], 6)
                    if u >= 2:
                        dve.wait_ge(S["rows"], u - 1)
                    for ih in range(2):
                        dve.wait_ge(S["scored"], 2 * u + ih + 1)
                        dve.tensor_reduce(colmax[:, u % 2, ih * 16:(ih + 1) * 16],
                                          score[u % 2][ih].rearrange("p (b i) -> p b i", i=32), AX, ALU.max,
                                          apply_transpose=True).then_inc(S["colmaxed"], 1)
                    continue
                if what == "rows":
                    u = k
                    dve.wait_ge(S["rows"], u + 1)
                    if u:
                        dve.wait_ge(S["shift_v"], u)
                    dve.tensor_reduce(rowmax[:], row_ps.rearrange("p (jh i) -> p i jh", jh=2), AX, ALU.max)\
                       .then_inc(S["rowmaxed"], 1)
                    dve.wait_ge(S["rowmaxed"], u + 1)
                    dve.tensor_copy(rowmax_h[:], rowmax[:]).then_inc(S["rowmax_h"], 1)
                    dve.wait_ge(S["rowmax_h"], u + 1)
                    if u >= 2:
                        dve.wait_ge(S["shift_x"], 2 * (u - 1))
                    dve.scalar_tensor_tensor(shift_v[:, u % 2, :], rowmax_h[:], minus_lo, rowmax[:],
                                             ALU.mult, ALU.add).then_inc(S["shift_v"], 1)
                    continue
                if len(item) < 3 or what in ("load", "load_x1"):
                    continue
                hf = item[2]
                c = 2 * k + hf
                cols = slice(hf * HT, (hf + 1) * HT)
                if what == "ln1":
                    dve.wait_ge(S["x_in"], 16 * (c + 1))
                    norm_stats(c, lambda t: x_in[:, t, :], stats, mv, "")
                    if c:
                        dve.wait_ge(S["xT_used"], c)
                    norm_apply(c, lambda t: x_in[:, t, :], mv, rstd, xn, "")
                elif what in ("q", "k"):
                    full_f, part, rest = (qf, q_part, r1q) if what == "q" else (kf, k_part, r1k)
                    dve.wait_ge(S[what + "f"], c + 1)
                    dve.wait_ge(S[what + "h"], c + 1)
                    if c:
                        dve.wait_ge(S[what + "l"], c)
                    dve.tensor_tensor(rest[:], full_f[:], part[:, 0, cols], ALU.subtract).then_inc(S["r1" + what], 1)
                    dve.wait_ge(S["r1" + what], c + 1)
                    if k and hf == 0:
                        dve.wait_ge(S[what + "_out"], 16 * k)
                    dve.tensor_copy(part[:, 1, cols], rest[:]).then_inc(S[what + "m"], 1)
                elif what == "norm":
                    dve.wait_ge(S["att"], NM * (k + 1))
                    sums = att[:, hf * TT:(hf + 1) * TT, :, :].rearrange("p n h (hpar v) -> p (n h hpar) v", hpar=2)
                    if c:
                        dve.wait_ge(S["attn_n"], 2 * c)
                    dve.reciprocal(rden[:], sums[:, :, DK]).then_inc(S["rden"], 1)
                    dve.wait_ge(S["rden"], c + 1)
                    if c >= 2:
                        dve.wait_ge(S["aT_used"], c - 1)
                    for hpar in range(2):
                        dve.scalar_tensor_tensor(
                            att_n[:, hf, :, :].rearrange("p n (hpar h d) -> p n hpar h d", hpar=2, d=DK)[:, :, hpar, :, :],
                            att[:, hf * TT:(hf + 1) * TT, :, hpar * VW:hpar * VW + DK], any_key[:, 2:3],
                            rden[:].rearrange("p (n h hpar) -> p n h hpar", n=TT, hpar=2)[:, :, :, hpar]
                            .unsqueeze(3).broadcast_to([128, TT, HP, DK]), ALU.mult, ALU.mult)\
                           .then_inc(S["attn_n"], 1)
                elif what == "proj":
                    bank, done = read_wait(dve, item)
                    dve.wait_ge(S["x_res"], 16 * (c + 1))
                    if c >= 2:
                        dve.wait_ge(stored[hf], 16 * k)
                    dve.tensor_tensor(x1[:, hf, :, :], bank.rearrange("p (n d) -> p n d", d=D),
                                      x_res[:], ALU.add).then_inc(S["x1"], 1)
                    dve.wait_ge(S["x1"], c + 1)
                    dve.sem_inc(done, 1)
                elif what == "ln2":
                    norm_stats(c, lambda t: x1[:, hf, t, :], stats2, mv2, "2")
                    if c:
                        dve.wait_ge(S["x2T"], c)
                    norm_apply(c, lambda t: x1[:, hf, t, :], mv2, rstd2, xn2, "2")
                elif what == "gate":
                    bank, done = read_wait(dve, item)
                    if c:
                        dve.wait_ge(S["onehot"], c)
                    dve.tensor_tensor(logit[:], bank[:, 0:TT * E].rearrange("p (n e) -> p n e", e=E),
                                      bg_row[:].unsqueeze(1).broadcast_to([128, TT, E]), ALU.add)\
                       .then_inc(S["logit"], 1)
                    dve.wait_ge(S["logit"], c + 1)
                    dve.sem_inc(done, 1)
                    dve.tensor_reduce(top[:], logit[:], AX, ALU.max).then_inc(S["top"], 1)
                    dve.wait_ge(S["top"], c + 1)
                    dve.tensor_tensor(is_top[:], logit[:], top[:].unsqueeze(2).broadcast_to([128, TT, E]),
                                      ALU.is_equal).then_inc(S["is_top"], 1)
                    dve.wait_ge(S["is_top"], c + 1)
                    dve.tensor_tensor(key[:], is_top[:], order.unsqueeze(1).broadcast_to([128, TT, E]),
                                      ALU.mult).then_inc(S["key"], 1)
                    dve.wait_ge(S["key"], c + 1)
                    dve.tensor_reduce(first[:], key[:], AX, ALU.max).then_inc(S["first"], 1)
                    dve.wait_ge(S["first"], c + 1)
                    if c:
                        dve.wait_ge(S["ohT"], c)
                    for s in range(3):
                        last = dve.tensor_tensor(onehot[:, :, s, :], key[:],
                                                 first[:].unsqueeze(2).broadcast_to([128, TT, E]), ALU.is_equal)
                    last.then_inc(S["onehot"], 1)
                elif what in ("up", "down") and item[3] % 2 == 0:
                    e = item[3]
                    pick(dve, S["picked_v"], what, c, e, (E // 2) * (2 * c + (what == "down")) + e // 2)
                elif what == "out":
                    bank, done = read_wait(dve, item)
                    dve.tensor_tensor(x1[:, hf, :, :], bank.rearrange("p (n d) -> p n d", d=D), x1[:, hf, :, :], ALU.add)\
                       .then_inc(S["y_out"], 1)
                    dve.wait_ge(S["y_out"], c + 1)
                    dve.sem_inc(done, 1)

        @block.tensor
        def _(pe):
            pe.wait_ge(S["consts"], 16 * N_CONST)
            pe.matmul(misc[0][:, 0:128], wp[:], pe_rev[:], start=True, stop=True).then_inc(full[0], 1)
            pe.wait_ge(S["masks_loaded"], 11)
            pe.wait_ge(S["ph_rev"], 1)
            pe.matmul(misc[1][0:H, 0:128], bias_heads[:], rev[:, 0, :], start=True, stop=True).then_inc(full[1], 1)

            def transposes(item, tiles, rows=128):
                bank, done = fill_wait(pe, item)
                for t in range(TT):
                    last = pe.transpose(bank[0:rows, t * 128:(t + 1) * 128], tiles(t), ident[:])
                return last, done

            def pv(v):
                g, m = divmod(v, NM)
                pe.wait_ge(S["prob"], 4 * (v + 1))
                pe.wait_ge(S["v_in"], 8 * (g + 1))
                pe.wait_ge(S["rowmaxed"], min(2 * v + 3, NU))
                if v:
                    pe.wait_ge(S["att"], v)
                for b in range(GB):
                    r = 64 * (b % 2)
                    for h2 in range(2):
                        at = ((b // 2) * 2 + h2) * 2 * VW
                        last = pe.matmul(pv_ps[r:r + 64, at:at + 2 * VW], prob[:, v % 2, h2 * GB + b, :],
                                         val[g % 2][:, b, 2 * m + h2, :], start=True, stop=True)
                last.then_inc(S["pv"], 1)

            for item in steps:
                what, k = item[0], item[1]
                if what == "scores":
                    u = k
                    v, ih = divmod(u, 2)
                    n, ml = divmod(v, NM // 2)
                    m = v % NM
                    if ih == 0 and ml == 0:
                        pe.wait_ge(q_in[n % 3], 16 * 4 * NS * (n // 3 + 1))
                        pe.wait_ge(k_in[n % 3], 16 * 2 * NS * (n // 3 + 1))
                    if u == 0:
                        pe.wait_ge(S["masks_loaded"], 14)
                        pe.wait_ge(S["pos_in"], 16 * (NS + 3))
                        pe.wait_ge(S["ones"], 16 * 3)
                    if u >= 2:
                        pe.wait_ge(S["prob"], 2 * (u - 1))
                    qs, ks = q_st[n % 3], k_st[n % 3]
                    for iq in range(2):
                        bank = score[u % 2][iq]
                        i0 = (2 * ih + iq) * IH
                        for hpar in range(2):
                            hq = 2 * hpar + ml
                            rows = bank[64 * hpar:64 * hpar + 64, :].rearrange("p (h2 b i) -> p h2 b i", h2=2, b=GB)
                            query = qs[:, hq, :, :].rearrange("p h2 (b t) -> p h2 b t", b=GB)
                            for b in range(GB):
                                pe.matmul(rows[:, :, b, :], ks[0:KC, hq, b * T:(b + 1) * T],
                                          query[0:KC, :, b, i0:i0 + IH], start=(b == 0), stop=False,
                                          skip_group_check=True)
                            for i in range(IH):
                                t = T - 1 - i0 - i
                                pe.matmul(rows[:, :, :, i], pos[0:KB, NM * hpar + m, t:t + T],
                                          query[0:KB, :, :, i0 + i], start=False, stop=False,
                                          skip_group_check=True)
                        pe.matmul(bank, mask_neg[:].rearrange("p a j -> p (a j)"),
                                  ident_h[0:64, i0:i0 + IH].unsqueeze(1).broadcast_to([64, 2 * GB, IH]),
                                  start=False, stop=True, skip_group_check=True).then_inc(S["scored"], 1)
                elif what == "rows":
                    u = k
                    pe.wait_ge(S["colmaxed"], 2 * (u + 1))
                    if u >= 3:
                        pe.wait_ge(S["att"], u // 2 - (1 - u % 2))
                    for h2 in range(2):
                        r = slice(64 * h2, 64 * h2 + 64)
                        for part in range(2):
                            o = slice(64 * h2 + 32 * part, 64 * h2 + 32 * part + 32)
                            last = pe.matmul(row_ps[o, :], colmax[r, u % 2, :], ident[r, r], start=True, stop=True)
                    last.then_inc(S["rows"], 1)
                elif what == "pv":
                    pv(k)
                elif what == "shift":
                    u = k
                    pe.wait_ge(S["shift_x"], 2 * (u + 1))
                    for ih in range(2):
                        last = pe.matmul(score[u % 2][ih], shift_sel[:], shift_x[:, u % 2, ih, :, :], start=False,
                                         stop=True, skip_group_check=True)
                    last.then_inc(S["shifted"], 1)
                elif what in ("load", "load_x1", "stack", "ln1", "ln2", "norm"):
                    pass
                else:
                    hf = item[2]
                    c = 2 * k + hf
                    if what == "xT":
                        pe.wait_ge(S["xn"], TT * (c + 1))
                        last, done = transposes(item, lambda t: xn[:, t, :])
                        last.then_inc(done, 1)
                        pe.wait_ge(done, turn[item] // 2 + 1)
                        pe.sem_inc(S["xT_used"], 1)
                    elif what == "cT":
                        pe.wait_ge(S["c_in"], 16 * (c + 1))
                        last, done = transposes(item, lambda t: c_in[:, t, :])
                        last.then_inc(done, 1)
                    elif what == "q":
                        bank, done = fill_wait(pe, item)
                        pe.wait_ge(S["xT"], c + 1)
                        pe.matmul(bank, wq[:], xT[:], start=True, stop=True).then_inc(done, 1)
                        pe.wait_ge(done, turn[item] // 2 + 1)
                        pe.sem_inc(S["q_done"], 1)
                    elif what == "k":
                        bank, done = fill_wait(pe, item)
                        pe.wait_ge(S["cT"], c + 1)
                        pe.matmul(bank, wk[:], cT[:], start=True, stop=True).then_inc(done, 1)
                    elif what == "v":
                        bank, done = fill_wait(pe, item)
                        for t in range(TT):
                            last = pe.matmul(bank[:, t * 128:(t + 1) * 128], cT[:, t * 128:(t + 1) * 128], wv[:],
                                             start=True, stop=True)
                        last.then_inc(done, 1)
                        pe.wait_ge(done, turn[item] // 2 + 1)
                        pe.sem_inc(S["cT_used"], 1)
                    elif what == "aT":
                        pe.wait_ge(S["attn_n"], 2 * (c + 1))
                        last, done = transposes(item, lambda t: att_n[:, hf, t, :])
                        last.then_inc(done, 1)
                        pe.wait_ge(done, turn[item] // 2 + 1)
                        pe.sem_inc(S["aT_used"], 1)
                    elif what == "proj":
                        bank, done = fill_wait(pe, item)
                        pe.wait_ge(S["aT"], c + 1)
                        for t in range(TT):
                            last = pe.matmul(bank[:, t * 128:(t + 1) * 128], aT[:, t * 128:(t + 1) * 128], wo[:],
                                             start=True, stop=True)
                        last.then_inc(done, 1)
                        pe.wait_ge(done, turn[item] // 2 + 1)
                        pe.sem_inc(S["proj_done"], 1)
                    elif what == "x2T":
                        pe.wait_ge(S["xn2"], TT * (c + 1))
                        last, done = transposes(item, lambda t: xn2[:, t, :])
                        last.then_inc(done, 1)
                    elif what == "gate":
                        bank, done = fill_wait(pe, item)
                        pe.wait_ge(S["x2T"], c + 1)
                        for t in range(TT):
                            last = pe.matmul(bank[:, t * E:(t + 1) * E], x2T[:, t * 128:(t + 1) * 128], wg[:],
                                             start=True, stop=True)
                        last.then_inc(done, 1)
                        pe.wait_ge(done, turn[item] // 2 + 1)
                        pe.sem_inc(S["gated"], 1)
                    elif what == "ohT":
                        pe.wait_ge(S["onehot"], c + 1)
                        last, done = transposes(item, lambda t: onehot[:, t, :, :].rearrange("p s e -> p (s e)"), 3 * E)
                        last.then_inc(done, 1)
                    elif what == "sel":
                        e = item[3]
                        bank, done = fill_wait(pe, item)
                        pe.wait_ge(S["ohT"], c + 1)
                        pe.matmul(bank, ident_h[0:E, e:e + 1].broadcast_to([E, 128]), ohT[0:E, :], start=True, stop=True).then_inc(done, 1)
                    elif what in ("up", "down"):
                        e = item[3]
                        n = (E // 2) * (2 * c + (what == "down")) + e // 2
                        pe.wait_ge(S["picked_p" if e % 2 else "picked_v"], n + 1)
                        if e == 0:
                            if what == "down":
                                pe.wait_ge(S["hid"], c + 1)
                            elif c:
                                pe.wait_ge(S["yT"], c)
                        pe.matmul(ffn_ps, (w1 if what == "up" else w2)[:, e, :], picked[:, 2 * (e % 2) + n % 2, :],
                                  start=(e == 0), stop=False).then_inc(S[what], 1)
                    elif what in ("gelu", "y"):
                        if c == 0 and what == "gelu":
                            pe.wait_ge(S["bias_in"], 48)
                        pe.matmul(ffn_ps, b12_rows[:, 0 if what == "gelu" else 1, :], ohT[:], start=False, stop=True)\
                          .then_inc(S["ffn_full"], 1)
                    elif what == "out":
                        pe.wait_ge(S["yT"], c + 1)
                        last, done = transposes(item, lambda t: yT[:, t * 128:(t + 1) * 128])
                        last.then_inc(done, 1)
                        pe.wait_ge(done, turn[item] // 2 + 1)
                        pe.sem_inc(S["yT_used"], 1)


def constants():
    import numpy as np
    ident = np.eye(128, dtype=np.float32)
    theta = np.arange(T, dtype=np.float32)[:, None] / np.float32(10000.0) ** (
        np.arange(0, D, 2, dtype=np.float32) / np.float32(D))
    enc = np.stack([np.sin(theta), np.cos(theta)], axis=-1).reshape(T, D)
    pe = np.zeros((D, 128), np.float32)
    pe[:, 0:T] = enc[::-1].T
    small = np.zeros((128, 64), np.float32)
    p = np.arange(128)
    small[p, p // DK] = 1.0
    part, own = p // 32 % 2, p % 32
    small[:, 16] = -1.0 * (part == 1)
    small[p, 17 + own] = 1.0
    small[:, 49:57] = E - np.arange(E)
    shift = np.where((p // 64)[:, None] == (p // 64)[None, :], -1.0, 0.0).astype(np.float32)
    ones = np.zeros((6, HP // 2, 2, GT), np.uint16)
    for row in range(6):
        ones[row, :, row % 2, :] = 0x3F80
    return {"c_ident": ident, "c_pe": pe, "c_small": small, "c_shift": shift, "c_ones": ones}


_INS = ["x", "ctx_1024", "mask_1xSxS2_bf1", "L0_xattn_w_q", "L0_xattn_w_k", "L0_xattn_w_v", "L0_xattn_w_p",
        "L0_xattn_w_o", "L0_xattn_b_u", "L0_xattn_b_v", "L0_ffn_Wg", "L0_ffn_bg", "L0_ffn_W1", "L0_ffn_b1",
        "L0_ffn_W2", "L0_ffn_b2"]


def kernel(**inputs):
    import numpy as _np
    import concourse.bacc as _bacc
    from concourse import mybir as _mybir
    from concourse.bass_utils import run_bass_kernel_spmd as _run

    nc = _bacc.Bacc("TRN2", target_bir_lowering=False, num_devices=1)
    arrays, args = {}, []

    def give(name, a):
        arrays[name] = a
        args.append(nc.dram_tensor(name, a.shape, _mybir.dt.from_np(a.dtype), kind="ExternalInput").ap())

    for name in _INS:
        a = _np.ascontiguousarray(inputs[name])
        give(f"in_{name}_dram", a.view(_np.uint8) if a.dtype == _np.bool_ else a)
    for name, a in constants().items():
        give(name, a)
    args.append(nc.dram_tensor("out_0_dram", (B, T, D), _mybir.dt.float32, kind="ExternalOutput").ap())
    xattn_moe_kernel(nc, *args)
    r = _run(nc, [arrays], core_ids=[0])
    return r.results[0]["out_0_dram"]
```

```python
from contextlib import ExitStack

import concourse.bass as bass
from concourse import mybir

F32 = mybir.dt.float32
BF16 = mybir.dt.bfloat16
U8 = mybir.dt.uint8
ALU = mybir.AluOpType
ACT = mybir.ActivationFunctionType
AX = mybir.AxisListType.X

B, T, D = 64, 64, 128
H, DK = 16, 8
HP = H // 2
E = 8
GB = 16
G = B // GB
GT = GB * T
HT = GT // 2
TT = HT // 128
NT = GT // 128
IH = 16
NM = H // 4
NQ = G * NM
NU = 2 * NQ
EPS = 1e-5
SCALE = float(DK) ** -0.5
NEG = 1e30
Q_PART = (0, 0, 0, 1, 1, 2)
K_PART = (0, 1, 2, 0, 1, 0)
NS = len(Q_PART)
RUNS_K = ((0, 3, 0, 1), (3, 2, 0, 1), (5, 1, 0, 1))
RUNS_Q = ((0, 3, 0, 0), (3, 2, 1, 0), (5, 1, 2, 0))
KC = NS * 2 * DK
KB = KC + 6
VW = DK + 1


def schedule():
    GAP = (0, None)

    def front(k):
        items = []
        for hf in range(2):
            items += [(0, ("load", k, hf)), (0, ("ln1", k, hf)), (9, ("cT", k, hf)), GAP, (9, ("xT", k, hf)),
                      (9, ("k", k, hf)), GAP, (9, ("q", k, hf)), (14, ("v", k, hf)), GAP]
        return items + [(0, ("stack", k))]

    def post(k):
        items = [(0, ("norm", k, hf)) for hf in range(2)] + [GAP]
        for hf in range(2):
            items += [(0, ("load_x1", k, hf)), (9, ("aT", k, hf)), GAP, (14, ("proj", k, hf)), (0, ("ln2", k, hf)),
                      GAP, GAP, (9, ("x2T", k, hf)), GAP, (5, ("gate", k, hf)), GAP, (5, ("ohT", k, hf)), GAP]
            items += [(3, ("sel", k, hf, e)) for e in range(3)]
            items += [(0, ("pick", k, hf, "up", e)) for e in range(2)] + [GAP]
            for e in range(E):
                if e + 3 < E:
                    items.append((3, ("sel", k, hf, e + 3)))
                if e + 2 < E:
                    items.append((0, ("pick", k, hf, "up", e + 2)))
                items.append((9, ("up", k, hf, e)))
            items.append((2, ("gelu", k, hf)))
            items += [(0, ("pick", k, hf, "down", e)) for e in range(2)] + [GAP]
            for e in range(E):
                if e + 2 < E:
                    items.append((0, ("pick", k, hf, "down", e + 2)))
                items.append((9, ("down", k, hf, e)))
            items += [(2, ("y", k, hf)), GAP, (9, ("out", k, hf))]
        return items

    def fill(out, items, share):
        cost = 0
        while items and cost < share:
            c, item = items.pop(0)
            if item is None:
                break
            out.append(item)
            cost += c

    def worth(items):
        return sum(c for c, _ in items)

    out = []
    for _, item in front(0):
        if item == ("xT", 0, 0):
            out.append(("setup", 0))
        if item == ("v", 0, 0):
            out.append(("zeros", 0))
        if item is not None:
            out.append(item)
    for g in range(G + 1):
        ahead = front(g + 1) if g + 1 < G else []
        behind = post(g - 1) if g else []
        if g == G:
            out += [("shift", NU - 1), ("pv", NQ - 1)] + [item for _, item in behind if item]
            break
        slots = 4 * NM
        for s in range(slots):
            u, half = 2 * NM * g + s // 2, s % 2
            out.append(("scores", u, half))
            if half == 0 and u % 2 and u >= 3:
                out.append(("pv", (u - 3) // 2))
            if half == 1 and u:
                out.append(("shift", u - 1))
            fill(out, ahead, worth(ahead) / max(slots * 3 // 4 - s, 1))
            if s >= 2:
                fill(out, behind, worth(behind) / (slots - s))
            if half == 1:
                out.append(("rows", u))
        out += [item for _, item in ahead + behind if item]
    return out


MISC = ("xT", "cT", "q", "k", "v", "aT", "proj", "x2T", "gate", "ohT", "sel", "out")


def xattn_moe_kernel(nc, x, ctx_in, mask, w_q, w_k, w_v, w_p, w_o, b_u, b_v, Wg, bg, W1, b1, W2, b2,
                     c_ident, c_pe, c_small, c_shift, c_perm, c_ones, out):
    steps = schedule()
    turn = {item: n for n, item in enumerate(i for i in steps if i[0] in MISC)}

    x_t = x.rearrange("(k b) t d -> k (b t) d", b=GB).rearrange("k (c n p) d -> (k c) p n d", c=2, p=128)
    c_t = ctx_in.rearrange("(k b) t d -> k (b t) d", b=GB).rearrange("k (c n p) d -> (k c) p n d", c=2, p=128)
    o_t = out.rearrange("(k b) t d -> k (b t) d", b=GB).rearrange("k (c n p) d -> (k c) p n d", c=2, p=128)
    q_dram = nc.dram_tensor("q_parts", (G, 3, D, GT), BF16, kind="Internal").ap()
    k_dram = nc.dram_tensor("k_parts", (G, 3, D, GT), BF16, kind="Internal").ap()
    p_dram = nc.dram_tensor("p_parts", (3, D, 128), BF16, kind="Internal").ap()
    c_dram = nc.dram_tensor("c_parts", (3, H, 128), BF16, kind="Internal").ap()

    ctx = ExitStack()
    with ctx:
        def sb(name, shape, dt=F32):
            return ctx.enter_context(nc.sbuf_tensor(name, shape, dt))

        def sem(name):
            return ctx.enter_context(nc.semaphore(name))

        ident = sb("ident", [128, 128])
        small = sb("small", [128, 64])
        head_of = small[:, 0:16]
        minus_lo = small[:, 16:17]
        shift_own = small[:, 17:49]
        order = small[:, 49:57]
        wq, wk, wv, wo = (sb(n, [128, 128]) for n in ("wq", "wk", "wv", "wo"))
        picked = sb("picked", [128, 4, HT])
        wq_in, wk_in, wp_in, wp = (picked[:, 0, 128 * i:128 * i + 128] for i in range(4))
        perm, pe_rev, shift_f = (picked[:, 1, 128 * i:128 * i + 128] for i in range(3))
        rev = picked[:, 2, 0:256].rearrange("p (a t) -> p a t", a=2)
        cst = picked[0:H, 3, 0:256].rearrange("p (a t) -> p a t", a=2)
        w1 = sb("w1", [128, E, 128])
        w2 = sb("w2", [128, E, 128])
        wg = sb("wg", [128, E])
        bg_row = sb("bg_row", [128, E])
        b_uv = sb("b_uv", [128, 2])
        b_perm = sb("b_perm", [128, 2])
        b12 = sb("b12", [E, 2, 128])
        mask_u = sb("mask_u", [128, 64], U8)
        mask_f = sb("mask_f", [128, 64])
        mask_neg = sb("mask_neg", [64, 2, 64], BF16)
        ident_h = sb("ident_h", [128, 128], BF16)
        shift_sel = sb("shift_sel", [128, 128], BF16)
        bias_diff = sb("bias_diff", [128, 1])
        bias_heads = sb("bias_heads", [128, H])
        any_key = sb("any_key", [128, 4])
        rev_part = sb("rev_part", [128, 3, 128], BF16)
        cst_part = sb("cst_part", [H, 3, 128], BF16)
        b12_rest = sb("b12_rest", [E, 2, 128])
        b12_part = sb("b12_part", [E, 2, 3, 128], BF16)
        b12_rows = sb("b12_rows", [3 * E, 2, 128], BF16)
        pos = sb("pos", [128, HP, 128], BF16)
        x_in = sb("x_in", [128, TT, D])
        c_in = sb("c_in", [128, TT, D])
        stats = sb("stats", [128, TT, 6])
        mv = sb("mv", [128, TT, 2])
        vare = sb("vare", [128, TT])
        rstd = sb("rstd", [128, TT])
        mhalf = sb("mhalf", [128, TT])
        xn = sb("xn", [128, TT, D])
        xT = sb("xT", [128, HT])
        cT = sb("cT", [128, HT])
        qf = sb("qf", [128, HT])
        kf = sb("kf", [128, HT])
        r1q = sb("r1q", [128, HT])
        r1k = sb("r1k", [128, HT])
        r1_of = {"q": r1q, "k": r1k}
        q_part = sb("q_part", [128, 3, GT], BF16)
        k_part = sb("k_part", [128, 3, GT], BF16)
        q_st = [sb(f"q_st{i}", [128, HP // 2, 2, GT], BF16) for i in range(3)]
        k_st = [sb(f"k_st{i}", [128, HP // 2, GT], BF16) for i in range(3)]
        val = [sb(f"val{i}", [128, GB, HP, 2 * VW]) for i in range(2)]
        colmax = sb("colmax", [128, 2, 32])
        rowmax = sb("rowmax", [128, 32])
        rowmax_h = sb("rowmax_h", [128, 32], BF16)
        shift_v = sb("shift_v", [128, 2, 32], BF16)
        shift_x = sb("shift_x", [128, 2, 2, 16, 32], BF16)
        prob = sb("prob", [128, 2, 2 * GB, T])
        att = sb("att", [128, NT, HP, 2 * VW])
        rden = sb("rden", [128, TT * H])
        att_n = sb("att_n", [128, 2, TT, D])
        x_res = sb("x_res", [128, TT, D])
        aT = sb("aT", [128, HT])
        x1 = sb("x1", [128, 2, TT, D])
        stats2 = sb("stats2", [128, TT, 6])
        mv2 = sb("mv2", [128, TT, 2])
        vare2 = sb("vare2", [128, TT])
        rstd2 = sb("rstd2", [128, TT])
        xn2 = sb("xn2", [128, TT, D])
        x2T = sb("x2T", [128, HT])
        logit = sb("logit", [128, TT, E])
        top = sb("top", [128, TT])
        first = sb("first", [128, TT])
        is_top = sb("is_top", [128, TT, E])
        key = sb("key", [128, TT, E])
        onehot = sb("onehot", [128, TT, 3, E])
        ohT = sb("ohT", [3 * E, HT], BF16)
        chosen = sb("chosen", [128, E, HT], BF16)
        hid = sb("hid", [128, HT])
        yT = sb("yT", [128, HT])

        ps = ctx.enter_context(nc.psum_tensor("ps", [128, 8, 512], F32))
        score = [[ps[:, 2 * p + ih, :] for ih in range(2)] for p in range(2)]
        row_ps = ps[:, 4, 0:64]
        pv_ps = ps[:, 4, 64:64 + NT * 4 * VW]
        ffn_ps = ps[:, 5, :]
        misc = [ps[:, 6, :], ps[:, 7, :]]

        names = """mhalf first_consts late_consts w_perm b_ps b_perm ones consts zeroed val_zeroed prep bias_heads rev ph_rev ph_cst rev_split cst_split bias_split p_out c_out pos_in bias_in
            x_in c_in stats mv vare rstd xn xT cT cT_used qf qh r1q qm ql kf kh r1k km kl q_out k_out q_in0 q_in1 q_in2 k_in0 k_in1 k_in2 v_in
            scored colmaxed rows rowmaxed rowmax_h shift_v shift_x shifted prob pv att
            rden attn_n aT x_res x1 stats2 mv2 vare2 rstd2 xn2 x2T logit top is_top key first onehot ohT
            chosen picked_v picked_p up down hid yT y_out stored0 stored1 full0 full1 free0 free1 ffn_full ffn_free proj_done
            xT_used q_done k_done gated hid_used yT_used aT_used""".split()
        S = {n: sem("s_" + n) for n in names}
        full = [S["full0"], S["full1"]]
        free = [S["free0"], S["free1"]]
        q_in = [S[f"q_in{i}"] for i in range(3)]
        k_in = [S[f"k_in{i}"] for i in range(3)]
        stored = [S["stored0"], S["stored1"]]
        N_CONST = 11

        def fill_wait(eng, item):
            n = turn[item] if isinstance(item, tuple) else item
            if n >= 2:
                eng.wait_ge(free[n % 2], n // 2)
            return misc[n % 2], full[n % 2]

        def read_wait(eng, item):
            n = turn[item] if isinstance(item, tuple) else item
            eng.wait_ge(full[n % 2], n // 2 + 1)
            return misc[n % 2], free[n % 2]

        def pick(eng, done, what, c, e, n):
            eng.wait_ge(S["chosen"], E * c + e + 1)
            if what == "up":
                eng.wait_ge(S["x2T"], c + 1)
                src = x2T
            else:
                eng.wait_ge(S["hid"], c + 1)
                src = hid
            if n >= 2:
                m = n - 2
                half, kind, i = m // E, (m // (E // 2)) % 2, m % (E // 2)
                eng.wait_ge(S[("up", "down")[kind]], E * half + 2 * i + e % 2 + 1)
            eng.tensor_tensor(picked[:, 2 * (e % 2) + n % 2, :], src[:], chosen[:, e, :], ALU.mult).then_inc(done, 1)

        block = ctx.enter_context(nc.Block())

        @block.sync
        def _(sp):
            for dst, src in ((ident[:], c_ident), (wq_in, w_q), (wk_in, w_k), (wv[:], w_v)):
                sp.dma_start(dst, src).then_inc(S["first_consts"], 16)
            sp.dma_start(x_in[:], x_t[0]).then_inc(S["x_in"], 16)
            sp.dma_start(c_in[:], c_t[0]).then_inc(S["c_in"], 16)
            for dst, src in ((small[:], c_small), (perm, c_perm),
                             (b_uv[:, 0:1], b_u.rearrange("h (d one) -> (h d) one", one=1)),
                             (b_uv[:, 1:2], b_v.rearrange("h (d one) -> (h d) one", one=1)),
                             (pe_rev, c_pe), (wp_in, w_p), (shift_f, c_shift),
                             (mask_u[0:64, :], mask[0]), (mask_u[64:128, :], mask[0]),
                             (b12[:, 0, :], b1), (b12[:, 1, :], b2)):
                sp.dma_start(dst, src).then_inc(S["consts"], 16)
            for i in range(3):
                sp.dma_start(q_st[i][KC:KB, :, :, :], c_ones.bitcast(BF16)).then_inc(S["ones"], 16)

            for item in steps:
                what, k = item[0], item[1]
                if what == "load":
                    c = 2 * k + item[2]
                    if c:
                        sp.wait_ge(S["xn"], c * TT)
                        sp.dma_start(x_in[:], x_t[c]).then_inc(S["x_in"], 16)
                        sp.wait_ge(S["cT"], c)
                        sp.dma_start(c_in[:], c_t[c]).then_inc(S["c_in"], 16)
                    if c == 1:
                        sp.wait_ge(S["rev_split"], 4)
                        sp.dma_start(p_dram.rearrange("s p t -> p s t"), rev_part[:]).then_inc(S["p_out"], 16)
                        sp.wait_ge(S["cst_split"], 4)
                        sp.dma_start(c_dram.rearrange("s h t -> h s t"), cst_part[:]).then_inc(S["c_out"], 16)
                        sp.wait_ge(S["bias_split"], 4)
                        for s in range(3):
                            sp.dma_start(b12_rows[s * E:(s + 1) * E, :, :], b12_part[:, :, s, :])\
                              .then_inc(S["bias_in"], 16)
                        sp.wait_ge(S["p_out"], 16)
                        for h2 in range(2):
                            for s, n_slot, part, step in RUNS_K:
                                r = (h2 * NS + s) * DK
                                for mh in range(2):
                                    src = p_dram[part:part + n_slot, 64 * mh + 32 * h2:64 * mh + 32 * h2 + 32]
                                    sp.dma_start(pos[r:r + n_slot * DK, 4 * mh:4 * mh + 4, :],
                                                 src.rearrange("s (d q) t -> s d q t", q=4))\
                                      .then_inc(S["pos_in"], 16)
                        sp.wait_ge(S["c_out"], 16)
                        sp.dma_start(pos[KC:KB, :, :], c_dram.rearrange("s (h2 q) t -> (s h2) q t", h2=2))\
                          .then_inc(S["pos_in"], 16)
                elif what == "stack":
                    sp.wait_ge(S["qh"], 2 * k + 2)
                    sp.wait_ge(S["qm"], 2 * k + 2)
                    sp.wait_ge(S["ql"], 2 * k + 2)
                    sp.dma_start(q_dram[k].rearrange("s p t -> p s t"), q_part[:]).then_inc(S["q_out"], 16)
                    sp.wait_ge(S["kh"], 2 * k + 2)
                    sp.wait_ge(S["km"], 2 * k + 2)
                    sp.wait_ge(S["kl"], 2 * k + 2)
                    sp.dma_start(k_dram[k].rearrange("s p t -> p s t"), k_part[:]).then_inc(S["k_out"], 16)
                    sp.wait_ge(S["q_out"], 16 * (k + 1))
                    sp.wait_ge(S["k_out"], 16 * (k + 1))
                    if k == 0:
                        sp.wait_ge(S["zeroed"], 3)
                    for m in range(2):
                        n = 2 * k + m
                        if n >= 3:
                            sp.wait_ge(S["scored"], 2 * NM * (n - 2))
                        for h2 in range(2):
                            rows = slice(64 * m + 32 * h2, 64 * m + 32 * h2 + 32)
                            for s, n_slot, part, _ in RUNS_K:
                                r = (h2 * NS + s) * DK
                                src = k_dram[k, part:part + n_slot, rows]
                                sp.dma_start(k_st[n % 3][r:r + n_slot * DK, :, :],
                                             src.rearrange("s (d q) t -> s d q t", q=4)).then_inc(k_in[n % 3], 16)
                            for s, n_slot, part, _ in RUNS_Q:
                                r = (h2 * NS + s) * DK
                                src = q_dram[k, part:part + 1, rows].broadcast_to([n_slot, 32, GT])
                                sp.dma_start(q_st[n % 3][r:r + n_slot * DK, :, h2, :],
                                             src.rearrange("s (d q) t -> s d q t", q=4)).then_inc(q_in[n % 3], 16)
                    if k == 0:
                        for dst, src in ((wo[:], w_o), (wg[:], Wg), (bg_row[:], bg.partition_broadcast(128)),
                                         (w1[:], W1.rearrange("e d i -> d e i")),
                                         (w2[:], W2.rearrange("e i d -> i e d"))):
                            sp.dma_start(dst, src).then_inc(S["late_consts"], 16)
                elif what == "load_x1":
                    c = 2 * k + item[2]
                    if c:
                        sp.wait_ge(S["x1"], c)
                    sp.dma_start(x_res[:], x_t[c]).then_inc(S["x_res"], 16)
                elif what == "out":
                    hf = item[2]
                    sp.wait_ge(S["y_out"], 2 * k + hf + 1)
                    sp.dma_start(o_t[2 * k + hf], x1[:, hf, :, :]).then_inc(stored[hf], 16)
            for hf in range(2):
                sp.wait_ge(stored[hf], 16 * G)

        @block.gpsimd
        def _(pool):
            pool.memset(mhalf[:], -0.5).then_inc(S["mhalf"], 1)

            def inverse_root(c, stat, variance, scaled, root, suffix):
                pool.wait_ge(S["mv" + suffix], TT * (c + 1))
                if c:
                    pool.wait_ge(S["rstd" + suffix], c)
                    pool.wait_ge(S["xn" + suffix], TT * c)
                pool.tensor_scalar(scaled[:], variance, EPS, None, ALU.add).then_inc(S["vare" + suffix], 1)
                pool.wait_ge(S["vare" + suffix], c + 1)
                if c == 0:
                    pool.wait_ge(S["mhalf"], 1)
                pool.tensor_tensor(root[:], scaled[:], mhalf[:], ALU.pow).then_inc(S["rstd" + suffix], 1)

            for item in steps:
                what, k = item[0], item[1]
                c = 2 * k + item[2] if len(item) > 2 else None
                if what == "ln1":
                    inverse_root(c, stats, mv[:, :, 1], vare, rstd, "")
                elif what == "ln2":
                    inverse_root(c, stats2, mv2[:, :, 1], vare2, rstd2, "2")
                elif what in ("q", "k"):
                    hf = item[2]
                    part = q_part if what == "q" else k_part
                    rest = r1_of[what]
                    pool.wait_ge(S[what + "m"], c + 1)
                    if k and hf == 0:
                        pool.wait_ge(S[what + "_out"], 16 * k)
                    pool.tensor_tensor(part[:, 2, hf * HT:(hf + 1) * HT], rest[:], part[:, 1, hf * HT:(hf + 1) * HT],
                                       ALU.subtract).then_inc(S[what + "l"], 1)
                elif what == "shift":
                    u = k
                    pool.wait_ge(S["shift_v"], u + 1)
                    if u >= 2:
                        pool.wait_ge(S["shifted"], u - 1)
                    for iq in range(2):
                        own = shift_own[:, iq * 16:(iq + 1) * 16]
                        pool.tensor_tensor(shift_x[:, u % 2, iq, :, :],
                                           shift_v[:, u % 2, :].unsqueeze(1).broadcast_to([128, 16, 32]),
                                           own.unsqueeze(2).broadcast_to([128, 16, 32]), ALU.mult)\
                            .then_inc(S["shift_x"], 1)
                elif what == "pick" and item[4] % 2:
                    kind, e = item[3:]
                    n = (E // 2) * (2 * c + (kind == "down")) + e // 2
                    pick(pool, S["picked_p"], kind, c, e, n)


        @block.scalar
        def _(act):
            for item in steps:
                what, k = item[0], item[1]
                if what == "shift":
                    u = k
                    act.wait_ge(S["shifted"], u + 1)
                    v, ih = divmod(u, 2)
                    if v >= 2:
                        act.wait_ge(S["pv"], v - 1)
                    for iq in range(2):
                        i = (2 * ih + iq) * IH
                        act.activation(prob[:, v % 2, :, i:i + IH], score[u % 2][iq].rearrange(
                            "p (hb i) -> p hb i", i=IH), ACT.Exp, scale=SCALE).then_inc(S["prob"], 1)
                    continue
                if what == "pv":
                    act.wait_ge(S["pv"], k + 1)
                    g, m = divmod(k, NM)
                    if m == 0 and g:
                        act.wait_ge(S["attn_n"], 4 * g)
                    act.activation(att[:, :, 2 * m:2 * m + 2, :].rearrange("p n h v -> p n (h v)"),
                                   pv_ps.rearrange("p (n v) -> p n v", v=4 * VW), ACT.Copy)\
                       .then_inc(S["att"], 1)
                    continue
                if len(item) < 3 or what in ("load", "load_x1"):
                    continue
                hf = item[2]
                c = 2 * k + hf
                cols = slice(hf * HT, (hf + 1) * HT)
                if what in ("xT", "cT"):
                    bank, done = read_wait(act, item)
                    if c:
                        act.wait_ge(S["q_done" if what == "xT" else "cT_used"], c)
                    act.activation((xT if what == "xT" else cT)[:], bank, ACT.Copy).then_inc(S[what], 1)
                    act.wait_ge(S[what], c + 1)
                    act.sem_inc(done, 1)
                elif what in ("q", "k"):
                    bank, done = read_wait(act, item)
                    full_f, part = (qf, q_part) if what == "q" else (kf, k_part)
                    if c:
                        act.wait_ge(S["r1" + what], c)
                    func, args = (ACT.Identity, {"bias": b_perm[:, 0:1]}) if what == "q" else (ACT.Copy, {})
                    if what == "q" and c == 0:
                        act.wait_ge(S["b_perm"], 1)
                    act.activation(full_f[:], bank, func, **args).then_inc(S[what + "f"], 1)
                    if k and hf == 0:
                        act.wait_ge(S[what + "_out"], 16 * k)
                    act.activation(part[:, 0, cols], bank, func, **args).then_inc(S[what + "h"], 1)
                    act.wait_ge(S[what + "h"], c + 1)
                    act.sem_inc(done, 1)
                elif what == "v" :
                    bank, done = read_wait(act, item)
                    if k >= 2:
                        act.wait_ge(S["pv"], NM * (k - 1))
                    if c == 0:
                        act.wait_ge(S["val_zeroed"], 6)
                    for bp in range(2):
                        for hpar in range(2):
                            dst = val[k % 2][64 * hpar:64 * hpar + 64, :, :, :].rearrange(
                                "p (n bp) h v -> p n bp h v", bp=2)[:, hf * TT:(hf + 1) * TT, bp, :,
                                                                    hpar * VW:hpar * VW + DK]
                            src = bank[64 * bp:64 * bp + 64, :].rearrange(
                                "p (n hpar h d) -> p n hpar h d", n=TT, hpar=2, d=DK)[:, :, hpar, :, :]
                            act.activation(dst, src, ACT.Copy).then_inc(S["v_in"], 1)
                    act.wait_ge(S["v_in"], 4 * (c + 1))
                    act.sem_inc(done, 1)
                elif what == "aT":
                    bank, done = read_wait(act, item)
                    if c:
                        act.wait_ge(S["proj_done"], c)
                    act.activation(aT[:], bank, ACT.Copy).then_inc(S["aT"], 1)
                    act.wait_ge(S["aT"], c + 1)
                    act.sem_inc(done, 1)
                elif what == "x2T":
                    bank, done = read_wait(act, item)
                    if c:
                        act.wait_ge(S["gated"], c)
                        act.wait_ge(S["picked_v"], E * (c - 1) + E // 2)
                        act.wait_ge(S["picked_p"], E * (c - 1) + E // 2)
                    act.activation(x2T[:], bank, ACT.Copy).then_inc(S["x2T"], 1)
                    act.wait_ge(S["x2T"], c + 1)
                    act.sem_inc(done, 1)
                elif what == "ohT":
                    bank, done = read_wait(act, item)
                    if c:
                        act.wait_ge(S["ffn_full"], 2 * c)
                    act.activation(ohT[:], bank[0:3 * E, :], ACT.Copy).then_inc(S["ohT"], 1)
                    act.wait_ge(S["ohT"], c + 1)
                    act.sem_inc(done, 1)
                elif what == "sel":
                    e = item[3]
                    bank, done = read_wait(act, item)
                    if c:
                        act.wait_ge(S["picked_p" if e % 2 else "picked_v"], E * (c - 1) + E // 2 + e // 2 + 1)
                    act.activation(chosen[:, e, :], bank, ACT.Copy).then_inc(S["chosen"], 1)
                    act.wait_ge(S["chosen"], E * c + e + 1)
                    act.sem_inc(done, 1)
                elif what == "gelu":
                    act.wait_ge(S["ffn_full"], 2 * c + 1)
                    if c:
                        act.wait_ge(S["picked_v"], E * c)
                        act.wait_ge(S["picked_p"], E * c)
                    act.activation(hid[:], ffn_ps, ACT.Gelu).then_inc(S["hid"], 1)
                elif what == "y":
                    act.wait_ge(S["ffn_full"], 2 * c + 2)
                    if c:
                        act.wait_ge(S["yT_used"], c)
                    act.activation(yT[:], ffn_ps, ACT.Copy).then_inc(S["yT"], 1)

        @block.vector
        def _(dve):
            dve.wait_ge(S["first_consts"], 16 * 4)

            def permute(dst, src):
                for hpar in range(2):
                    for mh in range(2):
                        o = dst[:, 64 * mh:64 * mh + 64].rearrange("k (r hpar ml) -> k hpar ml r", hpar=2, ml=2)
                        i = src[:, 64 * hpar + 32 * mh:64 * hpar + 32 * mh + 32].rearrange("k (ml r) -> k ml r", ml=2)
                        dve.tensor_copy(o[:, hpar, :, :], i).then_inc(S["w_perm"], 1)

            permute(wq, wq_in)
            permute(wk, wk_in)

            def setup():
                dve.wait_ge(S["consts"], 16 * N_CONST)
                permute(wp, wp_in)
                dve.wait_ge(S["b_ps"], 1)
                dve.tensor_copy(b_perm[:], score[0][0][:, 0:2]).then_inc(S["b_perm"], 1)
                dve.tensor_copy(ident_h[:], ident[:]).then_inc(S["prep"], 1)
                dve.tensor_copy(shift_sel[:], shift_f).then_inc(S["prep"], 1)
                dve.tensor_copy(mask_f[:], mask_u[:]).then_inc(S["prep"], 1)
                dve.wait_ge(S["b_perm"], 1)
                dve.tensor_tensor(bias_diff[:], b_perm[:, 1:2], b_perm[:, 0:1], ALU.subtract).then_inc(S["prep"], 1)
                dve.wait_ge(S["prep"], 4)
                dve.tensor_scalar(bias_heads[:], head_of, bias_diff[:, 0:1], None, ALU.mult)\
                   .then_inc(S["bias_heads"], 1)
                for h2 in range(2):
                    dve.tensor_scalar(mask_neg[:, h2, :], mask_f[0:64, :], 1.0, NEG, ALU.subtract, ALU.mult)\
                       .then_inc(S["prep"], 1)
                dve.tensor_reduce(any_key[:, 0:1], mask_f[:], AX, ALU.max).then_inc(S["prep"], 1)
                dve.wait_ge(S["prep"], 7)
                dve.reciprocal(any_key[:, 1:2], any_key[:, 0:1]).then_inc(S["prep"], 1)
                dve.wait_ge(S["prep"], 8)
                dve.tensor_tensor(any_key[:, 2:3], any_key[:, 0:1], any_key[:, 1:2], ALU.mult).then_inc(S["prep"], 1)
                dve.wait_ge(S["ph_rev"], 1)
                dve.tensor_copy(rev[:, 0, :], score[0][1][:, 0:128]).then_inc(S["rev"], 1)
                dve.wait_ge(S["rev"], 1)
                split(rev[:, 0, :], rev[:, 1, :], [rev_part[:, s, :] for s in range(3)], S["rev_split"], 0)
                dve.wait_ge(S["ph_cst"], 1)
                dve.tensor_copy(cst[:, 0, :], score[1][0][0:H, 0:128]).then_inc(S["rev"], 1)
                dve.wait_ge(S["rev"], 2)
                split(cst[:, 0, :], cst[:, 1, :], [cst_part[:, s, :] for s in range(3)], S["cst_split"], 0)
                split(b12[:], b12_rest[:], [b12_part[:, :, s, :] for s in range(3)], S["bias_split"], 0)

            def zeros():
                for i in range(3):
                    dve.memset(q_st[i][0:KC, :, :, :], 0.0).then_inc(S["zeroed"], 1)
                    if i < 2:
                        dve.memset(val[i][:], 0.0).then_inc(S["val_zeroed"], 1)
                        dve.wait_ge(S["val_zeroed"], 3 * i + 1)
                        for hpar in range(2):
                            dve.memset(val[i][64 * hpar:64 * hpar + 64, :, :, hpar * VW + DK], 1.0)\
                               .then_inc(S["val_zeroed"], 1)

            def split(whole, rest, parts, done, n):
                dve.tensor_copy(parts[0], whole).then_inc(done, 1)
                dve.wait_ge(done, n + 1)
                dve.tensor_tensor(rest, whole, parts[0], ALU.subtract).then_inc(done, 1)
                dve.wait_ge(done, n + 2)
                dve.tensor_copy(parts[1], rest).then_inc(done, 1)
                dve.wait_ge(done, n + 3)
                dve.tensor_tensor(parts[2], rest, parts[1], ALU.subtract).then_inc(done, 1)

            def norm_stats(c, tiles, stat, agg, suffix):
                if c:
                    dve.wait_ge(S["xn" + suffix], TT * c)
                    dve.wait_ge(S["rstd" + suffix], c)
                for t in range(TT):
                    dve.bn_stats(stat[:, t, :], tiles(t)).then_inc(S["stats" + suffix], 1)
                for t in range(TT):
                    dve.wait_ge(S["stats" + suffix], TT * c + t + 1)
                    dve.bn_aggr(agg[:, t, :], stat[:, t, :]).then_inc(S["mv" + suffix], 1)

            def norm_apply(c, tiles, agg, root, dst, suffix):
                dve.wait_ge(S["rstd" + suffix], c + 1)
                dve.wait_ge(S["mv" + suffix], TT * (c + 1))
                for t in range(TT):
                    dve.tensor_scalar(dst[:, t, :], tiles(t), agg[:, t, 0:1], root[:, t:t + 1],
                                      ALU.subtract, ALU.mult).then_inc(S["xn" + suffix], 1)

            for item in steps:
                what, k = item[0], item[1]
                if what == "setup":
                    setup()
                    continue
                if what == "zeros":
                    zeros()
                    continue
                if what == "scores":
                    u = k
                    if u >= 2:
                        dve.wait_ge(S["rows"], u - 1)
                    for ih in (item[2],):
                        dve.wait_ge(S["scored"], 2 * u + ih + 1)
                        dve.tensor_reduce(colmax[:, u % 2, ih * 16:(ih + 1) * 16],
                                          score[u % 2][ih].rearrange("p (b i) -> p b i", i=32), AX, ALU.max,
                                          apply_transpose=True).then_inc(S["colmaxed"], 1)
                    continue
                if what == "rows":
                    u = k
                    dve.wait_ge(S["rows"], u + 1)
                    if u:
                        dve.wait_ge(S["shift_v"], u)
                    dve.tensor_reduce(rowmax[:], row_ps.rearrange("p (jh i) -> p i jh", jh=2), AX, ALU.max)\
                       .then_inc(S["rowmaxed"], 1)
                    dve.wait_ge(S["rowmaxed"], u + 1)
                    dve.tensor_copy(rowmax_h[:], rowmax[:]).then_inc(S["rowmax_h"], 1)
                    dve.wait_ge(S["rowmax_h"], u + 1)
                    if u >= 2:
                        dve.wait_ge(S["shift_x"], 2 * (u - 1))
                    dve.scalar_tensor_tensor(shift_v[:, u % 2, :], rowmax_h[:], minus_lo, rowmax[:],
                                             ALU.mult, ALU.add).then_inc(S["shift_v"], 1)
                    continue
                if len(item) < 3 or what in ("load", "load_x1"):
                    continue
                hf = item[2]
                c = 2 * k + hf
                cols = slice(hf * HT, (hf + 1) * HT)
                if what == "ln1":
                    dve.wait_ge(S["x_in"], 16 * (c + 1))
                    norm_stats(c, lambda t: x_in[:, t, :], stats, mv, "")
                    if c:
                        dve.wait_ge(S["xT_used"], c)
                    norm_apply(c, lambda t: x_in[:, t, :], mv, rstd, xn, "")
                elif what in ("q", "k"):
                    full_f, part, rest = (qf, q_part, r1q) if what == "q" else (kf, k_part, r1k)
                    dve.wait_ge(S[what + "f"], c + 1)
                    dve.wait_ge(S[what + "h"], c + 1)
                    if c:
                        dve.wait_ge(S[what + "l"], c)
                    dve.tensor_tensor(rest[:], full_f[:], part[:, 0, cols], ALU.subtract).then_inc(S["r1" + what], 1)
                    dve.wait_ge(S["r1" + what], c + 1)
                    if k and hf == 0:
                        dve.wait_ge(S[what + "_out"], 16 * k)
                    dve.tensor_copy(part[:, 1, cols], rest[:]).then_inc(S[what + "m"], 1)
                elif what == "norm":
                    dve.wait_ge(S["att"], NM * (k + 1))
                    sums = att[:, hf * TT:(hf + 1) * TT, :, :].rearrange("p n h (hpar v) -> p (n h hpar) v", hpar=2)
                    if c:
                        dve.wait_ge(S["attn_n"], 2 * c)
                    dve.reciprocal(rden[:], sums[:, :, DK]).then_inc(S["rden"], 1)
                    dve.wait_ge(S["rden"], c + 1)
                    if c >= 2:
                        dve.wait_ge(S["aT_used"], c - 1)
                    for hpar in range(2):
                        dve.scalar_tensor_tensor(
                            att_n[:, hf, :, :].rearrange("p n (hpar h d) -> p n hpar h d", hpar=2, d=DK)[:, :, hpar, :, :],
                            att[:, hf * TT:(hf + 1) * TT, :, hpar * VW:hpar * VW + DK], any_key[:, 2:3],
                            rden[:].rearrange("p (n h hpar) -> p n h hpar", n=TT, hpar=2)[:, :, :, hpar]
                            .unsqueeze(3).broadcast_to([128, TT, HP, DK]), ALU.mult, ALU.mult)\
                           .then_inc(S["attn_n"], 1)
                elif what == "proj":
                    bank, done = read_wait(dve, item)
                    dve.wait_ge(S["x_res"], 16 * (c + 1))
                    if c >= 2:
                        dve.wait_ge(stored[hf], 16 * k)
                    dve.tensor_tensor(x1[:, hf, :, :], bank.rearrange("p (n d) -> p n d", d=D),
                                      x_res[:], ALU.add).then_inc(S["x1"], 1)
                    dve.wait_ge(S["x1"], c + 1)
                    dve.sem_inc(done, 1)
                elif what == "ln2":
                    norm_stats(c, lambda t: x1[:, hf, t, :], stats2, mv2, "2")
                    if c:
                        dve.wait_ge(S["x2T"], c)
                    norm_apply(c, lambda t: x1[:, hf, t, :], mv2, rstd2, xn2, "2")
                elif what == "gate":
                    bank, done = read_wait(dve, item)
                    if c:
                        dve.wait_ge(S["onehot"], c)
                    else:
                        dve.wait_ge(S["late_consts"], 16 * 5)
                    dve.tensor_tensor(logit[:], bank[:, 0:TT * E].rearrange("p (n e) -> p n e", e=E),
                                      bg_row[:].unsqueeze(1).broadcast_to([128, TT, E]), ALU.add)\
                       .then_inc(S["logit"], 1)
                    dve.wait_ge(S["logit"], c + 1)
                    dve.sem_inc(done, 1)
                    dve.tensor_reduce(top[:], logit[:], AX, ALU.max).then_inc(S["top"], 1)
                    dve.wait_ge(S["top"], c + 1)
                    dve.tensor_tensor(is_top[:], logit[:], top[:].unsqueeze(2).broadcast_to([128, TT, E]),
                                      ALU.is_equal).then_inc(S["is_top"], 1)
                    dve.wait_ge(S["is_top"], c + 1)
                    dve.tensor_tensor(key[:], is_top[:], order.unsqueeze(1).broadcast_to([128, TT, E]),
                                      ALU.mult).then_inc(S["key"], 1)
                    dve.wait_ge(S["key"], c + 1)
                    dve.tensor_reduce(first[:], key[:], AX, ALU.max).then_inc(S["first"], 1)
                    dve.wait_ge(S["first"], c + 1)
                    if c:
                        dve.wait_ge(S["ohT"], c)
                    for s in range(3):
                        last = dve.tensor_tensor(onehot[:, :, s, :], key[:],
                                                 first[:].unsqueeze(2).broadcast_to([128, TT, E]), ALU.is_equal)
                    last.then_inc(S["onehot"], 1)
                elif what == "pick" and item[4] % 2 == 0:
                    kind, e = item[3:]
                    pick(dve, S["picked_v"], kind, c, e, (E // 2) * (2 * c + (kind == "down")) + e // 2)
                elif what == "out":
                    bank, done = read_wait(dve, item)
                    dve.tensor_tensor(x1[:, hf, :, :], bank.rearrange("p (n d) -> p n d", d=D), x1[:, hf, :, :], ALU.add)\
                       .then_inc(S["y_out"], 1)
                    dve.wait_ge(S["y_out"], c + 1)
                    dve.sem_inc(done, 1)

        @block.tensor
        def _(pe):
            def setup():
                pe.wait_ge(S["consts"], 16 * N_CONST)
                pe.matmul(score[0][0][:, 0:2], perm, b_uv[:], start=True, stop=True).then_inc(S["b_ps"], 1)
                pe.wait_ge(S["w_perm"], 12)
                pe.matmul(score[0][1][:, 0:128], wp, pe_rev, start=True, stop=True).then_inc(S["ph_rev"], 1)
                pe.wait_ge(S["bias_heads"], 1)
                pe.wait_ge(S["rev"], 1)
                pe.matmul(score[1][0][0:H, 0:128], bias_heads[:], rev[:, 0, :], start=True, stop=True)\
                  .then_inc(S["ph_cst"], 1)

            def transposes(item, tiles, rows=128):
                bank, done = fill_wait(pe, item)
                for t in range(TT):
                    last = pe.transpose(bank[0:rows, t * 128:(t + 1) * 128], tiles(t), ident[:])
                return last, done

            def pv(v):
                g, m = divmod(v, NM)
                pe.wait_ge(S["prob"], 4 * (v + 1))
                pe.wait_ge(S["v_in"], 8 * (g + 1))
                pe.wait_ge(S["rowmaxed"], min(2 * v + 3, NU))
                if v:
                    pe.wait_ge(S["att"], v)
                for b in range(GB):
                    r = 64 * (b % 2)
                    for h2 in range(2):
                        at = ((b // 2) * 2 + h2) * 2 * VW
                        last = pe.matmul(pv_ps[r:r + 64, at:at + 2 * VW], prob[:, v % 2, h2 * GB + b, :],
                                         val[g % 2][:, b, 2 * m + h2, :], start=True, stop=True)
                last.then_inc(S["pv"], 1)

            for item in steps:
                what, k = item[0], item[1]
                if what == "setup":
                    setup()
                elif what == "scores":
                    u = k
                    v, ih = divmod(u, 2)
                    n, ml = divmod(v, NM // 2)
                    m = v % NM
                    if ih == 0 and ml == 0 and item[2] == 0:
                        pe.wait_ge(q_in[n % 3], 16 * 6 * (n // 3 + 1))
                        pe.wait_ge(k_in[n % 3], 16 * 6 * (n // 3 + 1))
                    if u == 0 and item[2] == 0:
                        pe.wait_ge(S["prep"], 7)
                        pe.wait_ge(S["rev"], 2)
                        pe.wait_ge(S["pos_in"], 16 * 13)
                        pe.wait_ge(S["ones"], 16 * 3)
                    if u >= 2:
                        pe.wait_ge(S["prob"], 2 * (u - 2) + item[2] + 1)
                    qs, ks = q_st[n % 3], k_st[n % 3]
                    for iq in (item[2],):
                        bank = score[u % 2][iq]
                        i0 = (2 * ih + iq) * IH
                        rows = [bank[64 * hpar:64 * hpar + 64, :].rearrange("p (h2 b i) -> p h2 b i", h2=2, b=GB)
                                for hpar in range(2)]
                        query = [qs[:, 2 * hpar + ml, :, :].rearrange("p h2 (b t) -> p h2 b t", b=GB)
                                 for hpar in range(2)]
                        for b in range(GB):
                            for hpar in range(2):
                                pe.matmul(rows[hpar][:, :, b, :], ks[0:KC, 2 * hpar + ml, b * T:(b + 1) * T],
                                          query[hpar][0:KC, :, b, i0:i0 + IH], start=(b == 0), stop=False,
                                          skip_group_check=True)
                        for i in range(IH):
                            t = T - 1 - i0 - i
                            for hpar in range(2):
                                pe.matmul(rows[hpar][:, :, :, i], pos[0:KB, 4 * (m // 2) + 2 * hpar + ml, t:t + T],
                                          query[hpar][0:KB, :, :, i0 + i], start=False, stop=False,
                                          skip_group_check=True)
                        pe.matmul(bank, mask_neg[:].rearrange("p a j -> p (a j)"),
                                  ident_h[0:64, i0:i0 + IH].unsqueeze(1).broadcast_to([64, 2 * GB, IH]),
                                  start=False, stop=True, skip_group_check=True).then_inc(S["scored"], 1)
                elif what == "rows":
                    u = k
                    pe.wait_ge(S["colmaxed"], 2 * (u + 1))
                    if u >= 3:
                        pe.wait_ge(S["att"], (u - 1) // 2)
                    for h2 in range(2):
                        r = slice(64 * h2, 64 * h2 + 64)
                        for part in range(2):
                            o = slice(64 * h2 + 32 * part, 64 * h2 + 32 * part + 32)
                            last = pe.matmul(row_ps[o, :], colmax[r, u % 2, :], ident[r, r], start=True, stop=True)
                    last.then_inc(S["rows"], 1)
                elif what == "pv":
                    pv(k)
                elif what == "shift":
                    u = k
                    pe.wait_ge(S["shift_x"], 2 * (u + 1))
                    for ih in range(2):
                        last = pe.matmul(score[u % 2][ih], shift_sel[:], shift_x[:, u % 2, ih, :, :], start=False,
                                         stop=True, skip_group_check=True)
                    last.then_inc(S["shifted"], 1)
                elif what in ("load", "load_x1", "stack", "ln1", "ln2", "norm", "zeros", "pick"):
                    pass
                else:
                    hf = item[2]
                    c = 2 * k + hf
                    if what == "xT":
                        pe.wait_ge(S["xn"], TT * (c + 1))
                        if c == 0:
                            pe.wait_ge(S["first_consts"], 16 * 4)
                        last, done = transposes(item, lambda t: xn[:, t, :])
                        last.then_inc(done, 1)
                        pe.wait_ge(done, turn[item] // 2 + 1)
                        pe.sem_inc(S["xT_used"], 1)
                    elif what == "cT":
                        pe.wait_ge(S["c_in"], 16 * (c + 1))
                        last, done = transposes(item, lambda t: c_in[:, t, :])
                        last.then_inc(done, 1)
                    elif what == "q":
                        bank, done = fill_wait(pe, item)
                        pe.wait_ge(S["xT"], c + 1)
                        if c == 0:
                            pe.wait_ge(S["w_perm"], 8)
                        pe.matmul(bank, wq[:], xT[:], start=True, stop=True).then_inc(done, 1)
                        pe.wait_ge(done, turn[item] // 2 + 1)
                        pe.sem_inc(S["q_done"], 1)
                    elif what == "k":
                        bank, done = fill_wait(pe, item)
                        pe.wait_ge(S["cT"], c + 1)
                        pe.matmul(bank, wk[:], cT[:], start=True, stop=True).then_inc(done, 1)
                    elif what == "v":
                        bank, done = fill_wait(pe, item)
                        for t in range(TT):
                            last = pe.matmul(bank[:, t * 128:(t + 1) * 128], cT[:, t * 128:(t + 1) * 128], wv[:],
                                             start=True, stop=True)
                        last.then_inc(done, 1)
                        pe.wait_ge(done, turn[item] // 2 + 1)
                        pe.sem_inc(S["cT_used"], 1)
                    elif what == "aT":
                        pe.wait_ge(S["attn_n"], 2 * (c + 1))
                        last, done = transposes(item, lambda t: att_n[:, hf, t, :])
                        last.then_inc(done, 1)
                        pe.wait_ge(done, turn[item] // 2 + 1)
                        pe.sem_inc(S["aT_used"], 1)
                    elif what == "proj":
                        bank, done = fill_wait(pe, item)
                        pe.wait_ge(S["aT"], c + 1)
                        if c == 0:
                            pe.wait_ge(S["late_consts"], 16 * 5)
                        for t in range(TT):
                            last = pe.matmul(bank[:, t * 128:(t + 1) * 128], aT[:, t * 128:(t + 1) * 128], wo[:],
                                             start=True, stop=True)
                        last.then_inc(done, 1)
                        pe.wait_ge(done, turn[item] // 2 + 1)
                        pe.sem_inc(S["proj_done"], 1)
                    elif what == "x2T":
                        pe.wait_ge(S["xn2"], TT * (c + 1))
                        last, done = transposes(item, lambda t: xn2[:, t, :])
                        last.then_inc(done, 1)
                    elif what == "gate":
                        bank, done = fill_wait(pe, item)
                        pe.wait_ge(S["x2T"], c + 1)
                        for t in range(TT):
                            last = pe.matmul(bank[:, t * E:(t + 1) * E], x2T[:, t * 128:(t + 1) * 128], wg[:],
                                             start=True, stop=True)
                        last.then_inc(done, 1)
                        pe.wait_ge(done, turn[item] // 2 + 1)
                        pe.sem_inc(S["gated"], 1)
                    elif what == "ohT":
                        pe.wait_ge(S["onehot"], c + 1)
                        last, done = transposes(item, lambda t: onehot[:, t, :, :].rearrange("p s e -> p (s e)"), 3 * E)
                        last.then_inc(done, 1)
                    elif what == "sel":
                        e = item[3]
                        bank, done = fill_wait(pe, item)
                        pe.wait_ge(S["ohT"], c + 1)
                        pe.matmul(bank, ident_h[0:E, e:e + 1].broadcast_to([E, 128]), ohT[0:E, :], start=True, stop=True).then_inc(done, 1)
                    elif what in ("up", "down"):
                        e = item[3]
                        n = (E // 2) * (2 * c + (what == "down")) + e // 2
                        pe.wait_ge(S["picked_p" if e % 2 else "picked_v"], n + 1)
                        if e == 0:
                            if what == "down":
                                pe.wait_ge(S["hid"], c + 1)
                            elif c:
                                pe.wait_ge(S["yT"], c)
                        pe.matmul(ffn_ps, (w1 if what == "up" else w2)[:, e, :], picked[:, 2 * (e % 2) + n % 2, :],
                                  start=(e == 0), stop=False).then_inc(S[what], 1)
                    elif what in ("gelu", "y"):
                        if c == 0 and what == "gelu":
                            pe.wait_ge(S["bias_in"], 48)
                        pe.matmul(ffn_ps, b12_rows[:, 0 if what == "gelu" else 1, :], ohT[:], start=False, stop=True)\
                          .then_inc(S["ffn_full"], 1)
                    elif what == "out":
                        pe.wait_ge(S["yT"], c + 1)
                        last, done = transposes(item, lambda t: yT[:, t * 128:(t + 1) * 128])
                        last.then_inc(done, 1)
                        pe.wait_ge(done, turn[item] // 2 + 1)
                        pe.sem_inc(S["yT_used"], 1)


def constants():
    import numpy as np
    ident = np.eye(128, dtype=np.float32)
    theta = np.arange(T, dtype=np.float32)[:, None] / np.float32(10000.0) ** (
        np.arange(0, D, 2, dtype=np.float32) / np.float32(D))
    enc = np.stack([np.sin(theta), np.cos(theta)], axis=-1).reshape(T, D)
    pe = np.zeros((D, 128), np.float32)
    pe[:, 0:T] = enc[::-1].T
    small = np.zeros((128, 64), np.float32)
    p = np.arange(128)
    mh, h2, d, hpar, ml = p // 64, p // 32 % 2, p // 4 % 8, p // 2 % 2, p % 2
    perm = np.zeros((128, 128), np.float32)
    perm[((hpar * 2 + mh) * 2 + ml) * 16 + h2 * 8 + d, p] = 1.0
    small[p, h2 * 8 + mh * 4 + hpar * 2 + ml] = 1.0
    part, own = p // 32 % 2, p % 32
    small[:, 16] = -1.0 * (part == 1)
    small[p, 17 + own] = 1.0
    small[:, 49:57] = E - np.arange(E)
    shift = np.where((p // 64)[:, None] == (p // 64)[None, :], -1.0, 0.0).astype(np.float32)
    ones = np.zeros((6, HP // 2, 2, GT), np.uint16)
    for row in range(6):
        ones[row, :, row % 2, :] = 0x3F80
    return {"c_ident": ident, "c_pe": pe, "c_small": small, "c_shift": shift, "c_perm": perm, "c_ones": ones}


_INS = ["x", "ctx_1024", "mask_1xSxS2_bf1", "L0_xattn_w_q", "L0_xattn_w_k", "L0_xattn_w_v", "L0_xattn_w_p",
        "L0_xattn_w_o", "L0_xattn_b_u", "L0_xattn_b_v", "L0_ffn_Wg", "L0_ffn_bg", "L0_ffn_W1", "L0_ffn_b1",
        "L0_ffn_W2", "L0_ffn_b2"]


def kernel(**inputs):
    import numpy as _np
    import concourse.bacc as _bacc
    from concourse import mybir as _mybir
    from concourse.bass_utils import run_bass_kernel_spmd as _run

    nc = _bacc.Bacc("TRN2", target_bir_lowering=False, num_devices=1)
    arrays, args = {}, []

    def give(name, a):
        arrays[name] = a
        args.append(nc.dram_tensor(name, a.shape, _mybir.dt.from_np(a.dtype), kind="ExternalInput").ap())

    for name in _INS:
        a = _np.ascontiguousarray(inputs[name])
        give(f"in_{name}_dram", a.view(_np.uint8) if a.dtype == _np.bool_ else a)
    for name, a in constants().items():
        give(name, a)
    args.append(nc.dram_tensor("out_0_dram", (B, T, D), _mybir.dt.float32, kind="ExternalOutput").ap())
    xattn_moe_kernel(nc, *args)
    r = _run(nc, [arrays], core_ids=[0])
    return r.results[0]["out_0_dram"]
```

```python
from contextlib import ExitStack

import concourse.bass as bass
from concourse import mybir

F32 = mybir.dt.float32
BF16 = mybir.dt.bfloat16
U8 = mybir.dt.uint8
ALU = mybir.AluOpType
ACT = mybir.ActivationFunctionType
AX = mybir.AxisListType.X

B, T, D = 64, 64, 128
H, DK = 16, 8
HP = H // 2
E = 8
GB = 16
G = B // GB
GT = GB * T
HT = GT // 2
TT = HT // 128
NT = GT // 128
IH = T // 2
NM = H // 4
NQ = G * NM
NU = 2 * NQ
EPS = 1e-5
SCALE = float(DK) ** -0.5
NEG = 1e30
Q_PART = (0, 0, 0, 1, 1, 2)
K_PART = (0, 1, 2, 0, 1, 0)
NS = len(Q_PART)
RUNS_K = ((0, 3, 0), (3, 2, 0), (5, 1, 0))
RUNS_Q = ((0, 3, 0), (3, 2, 1), (5, 1, 2))
KC = NS * 2 * DK
KB = KC + 6
VW = DK + 1


def schedule():
    GAP = (0, None)

    def front(k):
        items = [(0, ("load", 0, 0))] if k == 0 else []
        for hf in range(2):
            items += [(0, ("stats1", k, hf)), (9, ("cT", k, hf)), GAP, (0, ("ln1", k, hf)), GAP,
                      (9, ("xT", k, hf))]
            if (k, hf) != (G - 1, 1):
                items.append((0, ("load", k + hf, 1 - hf)))
            items += [(9, ("k", k, hf)), GAP, (0, ("split", k, hf, "k")), (9, ("q", k, hf)), (14, ("v", k, hf, 0)),
                      (0, ("split", k, hf, "q")), (0, ("parts", k, hf)), (14, ("v", k, hf, 1)), GAP]
        return items + [(0, ("stack", k))]

    def post(k):
        items = [(0, ("norm", k, hf)) for hf in range(2)]
        items += [GAP, (0, ("load_x1", k, 0)), (9, ("aT", k, 0)), GAP, (14, ("proj", k, 0)), (0, ("stats2", k, 0)),
                  GAP, (0, ("ln2", k, 0)), GAP, (9, ("x2T", k, 0)), GAP, (5, ("gate", k, 0)), GAP]
        for hf in range(2):
            between = {} if hf else {
                ("up", 1): [(0, ("load_x1", k, 1)), (9, ("aT", k, 1))], ("up", 3): [(14, ("proj", k, 1))],
                ("up", 4): [(0, ("stats2", k, 1))], ("up", 5): [(0, ("ln2", k, 1))],
                ("gelu", 0): [(9, ("x2T", k, 1))], ("down", 1): [(5, ("gate", k, 1))],
                ("down", 4): [(5, ("ohT", k, 1))], ("down", 6): [(0, ("spread", k, 1, 0))]}
            if hf:
                items += [(0, ("spread", k, 1, 1)), (9, ("out", k, 0)), GAP]
            else:
                items += [(5, ("ohT", k, 0)), GAP, (0, ("spread", k, 0, 0)), (0, ("spread", k, 0, 1)), GAP]
            items += [(0, ("pick", k, hf, "up", e)) for e in range(2)]
            for e in range(E):
                if e + 2 < E:
                    items.append((0, ("pick", k, hf, "up", e + 2)))
                items.append((9, ("up", k, hf, e)))
                items += between.get(("up", e), [])
            items.append((2, ("gelu", k, hf)))
            items += [(0, ("pick", k, hf, "down", e)) for e in range(2)]
            items += between.get(("gelu", 0), [GAP])
            for e in range(E):
                if e + 2 < E:
                    items.append((0, ("pick", k, hf, "down", e + 2)))
                items.append((9, ("down", k, hf, e)))
                items += between.get(("down", e), [])
            items += [(2, ("y", k, hf)), GAP]
        items.append((9, ("out", k, 1)))
        return items

    def fill(out, items, share):
        cost = 0
        while items and cost < share:
            c, item = items.pop(0)
            if item is None:
                break
            out.append(item)
            cost += c

    def worth(items):
        return sum(c for c, _ in items)

    out = []
    for _, item in front(0):
        if item == ("xT", 0, 0):
            out.append(("setup", 0))
        if item == ("split", 0, 0, "k"):
            out.append(("tables", 0))
        if item is not None:
            out.append(item)
    for g in range(G + 1):
        ahead = front(g + 1) if g + 1 < G else []
        behind = post(g - 1) if g else []
        if g == G:
            out += [("shift", NU - 1)] + [("pv", NQ - 1, part) for part in range(4)]
            out += [item for _, item in behind if item]
            break
        slots = 4 * NM
        for s in range(slots):
            u, half = 2 * NM * g + s // 2, s % 2
            out.append(("scores", u, half))
            if half == 1 and u:
                out.append(("shift", u - 1))
            others = []
            fill(others, ahead, worth(ahead) / max(slots * 3 // 4 - s, 1))
            if s >= 3:
                fill(others, behind, worth(behind) / (slots - s))
            if half == 0 and u % 2 and u >= 3:
                for part in range(4):
                    out.append(("pv", (u - 3) // 2, part))
                    n = (len(others) + 3 - part) // (4 - part)
                    out += others[:n]
                    others = others[n:]
            out += others
            if half == 1:
                out.append(("rows", u))
        out += [item for _, item in ahead + behind if item]
    return out


MISC = ("xT", "cT", "q", "k", "v", "aT", "proj", "x2T", "gate", "ohT", "out")


def xattn_moe_kernel(nc, x, ctx_in, mask, w_q, w_k, w_v, w_p, w_o, b_u, b_v, Wg, bg, W1, b1, W2, b2,
                     c_ident, c_pe, c_small, c_shift, c_perm, c_ones, out):
    steps = schedule()
    turn = {item: n for n, item in enumerate(i for i in steps if i[0] in MISC)}

    x_t = x.rearrange("(k b) t d -> k (b t) d", b=GB).rearrange("k (c n p) d -> (k c) p n d", c=2, p=128)
    c_t = ctx_in.rearrange("(k b) t d -> k (b t) d", b=GB).rearrange("k (c n p) d -> (k c) p n d", c=2, p=128)
    o_t = out.rearrange("(k b) t d -> k (b t) d", b=GB).rearrange("k (c n p) d -> (k c) p n d", c=2, p=128)
    q_dram = nc.dram_tensor("q_parts", (G, 3, D, GT), BF16, kind="Internal").ap()
    k_dram = nc.dram_tensor("k_parts", (G, 3, D, 2 * GT), BF16, kind="Internal").ap()
    p_dram = nc.dram_tensor("p_parts", (3, D, 2 * 128), BF16, kind="Internal").ap()
    c_dram = nc.dram_tensor("c_parts", (3, H, 2 * 128), BF16, kind="Internal").ap()

    o_dram = nc.dram_tensor("onehot_rows", (2 * G, E, HT), BF16, kind="Internal").ap()

    ctx = ExitStack()
    with ctx:
        def sb(name, shape, dt=F32):
            return ctx.enter_context(nc.sbuf_tensor(name, shape, dt))

        def sem(name):
            return ctx.enter_context(nc.semaphore(name))

        ident = sb("ident", [128, 128])
        small = sb("small", [128, 64])
        head_of = small[:, 0:16]
        minus_lo = small[:, 16:17]
        shift_own = small[:, 17:49]
        order = small[:, 49:57]
        row_of = small[:, 57:59]
        parity = small[:, 59:61]
        wq, wk, wv, wo = (sb(n, [128, 128]) for n in ("wq", "wk", "wv", "wo"))
        picked = sb("picked", [128, 4, HT])
        wq_in, wk_in, wp_in, wp = (picked[:, 0, 128 * i:128 * i + 128] for i in range(4))
        perm, pe_rev, shift_f = (picked[:, 1, 128 * i:128 * i + 128] for i in range(3))
        rev = picked[:, 2, :].rearrange("p (a t) -> p a t", a=2)
        cst = picked[0:H, 3, :].rearrange("p (a t) -> p a t", a=2)
        w1 = sb("w1", [128, E, 128])
        w2 = sb("w2", [128, E, 128])
        wg = sb("wg", [128, E])
        bg_row = sb("bg_row", [128, E])
        b_uv = sb("b_uv", [128, 2])
        b_perm = sb("b_perm", [128, 2])
        b12 = sb("b12", [E, 2, 128])
        mask_u = sb("mask_u", [128, 64], U8)
        mask_f = sb("mask_f", [128, 64])
        mask_neg = sb("mask_neg", [64, 64, 2], BF16)
        ident_h = sb("ident_h", [128, 128], BF16)
        shift_sel = sb("shift_sel", [128, 128], BF16)
        bias_diff = sb("bias_diff", [128, 1])
        bias_heads = sb("bias_heads", [128, H])
        any_key = sb("any_key", [128, 4])
        rev_part = sb("rev_part", [128, 3, 256], BF16)
        cst_part = sb("cst_part", [H, 3, 256], BF16)
        b12_rest = sb("b12_rest", [E, 2, 128])
        b12_part = sb("b12_part", [E, 2, 3, 128], BF16)
        b12_rows = sb("b12_rows", [3 * E, 2, 128], BF16)
        pos = sb("pos", [128, HP, 256], BF16)
        x_in = sb("x_in", [128, TT, D])
        c_in = sb("c_in", [128, TT, D])
        stats = sb("stats", [128, TT, 6])
        mv = sb("mv", [128, TT, 2])
        vare = sb("vare", [128, TT])
        rstd = sb("rstd", [128, TT])
        mhalf = sb("mhalf", [128, TT])
        xT = sb("xT", [128, HT])
        cT = sb("cT", [128, HT, 2])
        qf = sb("qf", [128, HT])
        kf = sb("kf", [128, HT, 2])
        q_part = sb("q_part", [128, 3, HT], BF16)
        k_part = sb("k_part", [128, 3, 2 * HT], BF16)
        parts_of = {"q": (qf[:], q_part), "k": (kf[:].rearrange("p j x -> p (j x)"), k_part)}
        q_st = [sb(f"q_st{i}", [128, HP // 2, GT], BF16) for i in range(3)]
        k_st = [sb(f"k_st{i}", [128, HP // 2, 2 * GT], BF16) for i in range(3)]
        val = [sb(f"val{i}", [128, GB, HP, 2 * VW]) for i in range(2)]
        turned = sb("turned", [128, 512])
        colmax = sb("colmax", [128, 2, 2, GB, 2])
        rowmax = sb("rowmax", [128, 32])
        rowmax_h = sb("rowmax_h", [128, 32], BF16)
        shift_v = sb("shift_v", [128, 2, 32], BF16)
        shift_x = sb("shift_x", [128, 2, 2, GB, IH], BF16)
        prob = sb("prob", [128, 2, 2 * GB, T])
        att = sb("att", [128, NT, HP, 2 * VW])
        rden = sb("rden", [128, TT * H])
        att_n = sb("att_n", [128, 2, TT, D])
        aT = sb("aT", [128, HT])
        x1 = sb("x1", [128, 2, TT, D])
        stats2 = sb("stats2", [128, TT, 6])
        mv2 = sb("mv2", [128, TT, 2])
        vare2 = sb("vare2", [128, TT])
        rstd2 = sb("rstd2", [128, TT])
        xn2 = sb("xn2", [128, TT, D])
        x2T = sb("x2T", [128, HT])
        logit = sb("logit", [128, TT, E])
        top = sb("top", [128, TT])
        first = sb("first", [128, TT])
        is_top = sb("is_top", [128, TT, E])
        key = sb("key", [128, TT, E])
        onehot = sb("onehot", [128, TT, 3, E])
        ohT = sb("ohT", [3 * E, 2, HT], BF16)
        chosen = sb("chosen", [128, E, HT], BF16)
        hid = sb("hid", [128, HT])
        yT = sb("yT", [128, HT])

        ps = ctx.enter_context(nc.psum_tensor("ps", [128, 8, 512], F32))
        score = [[ps[:, 2 * p + h2, :] for h2 in range(2)] for p in range(2)]
        row_ps = ps[:, 4, 0:128]
        pv_ps = ps[:, 4, 128:128 + NT * 4 * VW]
        ffn_ps = ps[:, 5, :]
        misc = [ps[:, 6, :], ps[:, 7, :]]

        names = """mhalf first_consts late_consts turned w_perm b_ps b_perm ones consts val_ones prep bias_heads rev
            ph_rev ph_cst rev_split cst_split bias_split p_out c_out pos_in bias_in x_in c_in stats mv vare
            rstd xn xT cT cT_used qf qh r1q qm ql kf kh r1k km kl q_out k_out q_in0 q_in1 q_in2 k_in0 k_in1
            k_in2 v_in scored colmaxed rows rowmaxed rowmax_h shift_v shift_xv shift_xp shifted prob pv att
            rden attn_n aT x_res x1 stats2 mv2 vare2 rstd2 xn2 x2T logit top is_top key first onehot ohT
            chosen_in0 chosen_in1 oh_out picked_v picked_p up down hid yT y_out stored0 stored1 full0 full1
            free0 free1 ffn_full proj_done xT_used q_done gated yT_used aT_used""".split()
        S = {n: sem("s_" + n) for n in names}
        full = [S["full0"], S["full1"]]
        free = [S["free0"], S["free1"]]
        q_in = [S[f"q_in{i}"] for i in range(3)]
        k_in = [S[f"k_in{i}"] for i in range(3)]
        chosen_in = [S["chosen_in0"], S["chosen_in1"]]
        stored = [S["stored0"], S["stored1"]]
        N_CONST = 11

        def fill_wait(eng, item):
            n = turn[item] if isinstance(item, tuple) else item
            if n >= 2:
                eng.wait_ge(free[n % 2], n // 2)
            return misc[n % 2], full[n % 2]

        def read_wait(eng, item):
            n = turn[item] if isinstance(item, tuple) else item
            eng.wait_ge(full[n % 2], n // 2 + 1)
            return misc[n % 2], free[n % 2]

        def pick(eng, done, what, c, e, n):
            eng.wait_ge(chosen_in[e // (E // 2)], 16 * (c + 1))
            if what == "up":
                eng.wait_ge(S["x2T"], c + 1)
                src = x2T
            else:
                eng.wait_ge(S["hid"], c + 1)
                src = hid
            if n >= 2:
                m = n - 2
                half, kind, i = m // E, (m // (E // 2)) % 2, m % (E // 2)
                eng.wait_ge(S[("up", "down")[kind]], E * half + 2 * i + e % 2 + 1)
            eng.tensor_tensor(picked[:, 2 * (e % 2) + n % 2, :], src[:], chosen[:, e, :], ALU.mult).then_inc(done, 1)

        def expand(eng, u, h2, done):
            eng.wait_ge(S["shift_v"], u + 1)
            if u >= 2:
                eng.wait_ge(S["shifted"], u - 1)
            eng.tensor_tensor(shift_x[:, u % 2, h2, :, :], shift_v[:, u % 2, :].unsqueeze(1).broadcast_to([128, GB, IH]),
                              shift_own[:, h2 * GB:(h2 + 1) * GB].unsqueeze(2).broadcast_to([128, GB, IH]),
                              ALU.mult).then_inc(done, 1)

        block = ctx.enter_context(nc.Block())

        @block.sync
        def _(sp):
            for dst, src in ((ident[:], c_ident), (wq_in, w_q), (wk_in, w_k), (wv[:], w_v)):
                sp.dma_start(dst, src).then_inc(S["first_consts"], 16)
            sp.dma_start(x_in[:], x_t[0]).then_inc(S["x_in"], 16)
            sp.dma_start(c_in[:], c_t[0]).then_inc(S["c_in"], 16)
            for dst, src in ((small[:], c_small), (perm, c_perm),
                             (b_uv[:, 0:1], b_u.rearrange("h (d one) -> (h d) one", one=1)),
                             (b_uv[:, 1:2], b_v.rearrange("h (d one) -> (h d) one", one=1)),
                             (pe_rev, c_pe), (wp_in, w_p), (shift_f, c_shift),
                             (mask_u[0:64, :], mask[0]), (mask_u[64:128, :], mask[0]),
                             (b12[:, 0, :], b1), (b12[:, 1, :], b2)):
                sp.dma_start(dst, src).then_inc(S["consts"], 16)
            for i in range(3):
                sp.dma_start(q_st[i][KC:KB, :, :], c_ones.bitcast(BF16)).then_inc(S["ones"], 16)

            for item in steps:
                what, k = item[0], item[1]
                if what == "load":
                    c = 2 * k + item[2]
                    if c:
                        sp.wait_ge(S["cT"], c)
                        sp.dma_start(c_in[:], c_t[c]).then_inc(S["c_in"], 16)
                        sp.wait_ge(S["xT_used"], c)
                        sp.dma_start(x_in[:], x_t[c]).then_inc(S["x_in"], 16)
                elif what == "tables":
                    sp.wait_ge(S["rev_split"], 4)
                    sp.dma_start(p_dram.rearrange("s p t -> p s t"), rev_part[:]).then_inc(S["p_out"], 16)
                    sp.wait_ge(S["cst_split"], 4)
                    sp.dma_start(c_dram.rearrange("s h t -> h s t"), cst_part[:]).then_inc(S["c_out"], 16)
                    sp.wait_ge(S["bias_split"], 4)
                    for s in range(3):
                        sp.dma_start(b12_rows[s * E:(s + 1) * E, :, :], b12_part[:, :, s, :])\
                          .then_inc(S["bias_in"], 16)
                    sp.wait_ge(S["p_out"], 16)
                    for hpar in range(2):
                        for s, n_slot, part in RUNS_K:
                            r = (hpar * NS + s) * DK
                            for mh in range(2):
                                src = p_dram[part:part + n_slot, 64 * mh + 32 * hpar:64 * mh + 32 * hpar + 32]
                                sp.dma_start(pos[r:r + n_slot * DK, 4 * mh:4 * mh + 4, :],
                                             src.rearrange("s (d q) t -> s d q t", q=4))\
                                  .then_inc(S["pos_in"], 16)
                    sp.wait_ge(S["c_out"], 16)
                    sp.dma_start(pos[KC:KB, :, :], c_dram.rearrange("s (hpar q) t -> (s hpar) q t", hpar=2))\
                      .then_inc(S["pos_in"], 16)
                elif what == "parts":
                    hf = item[2]
                    c = 2 * k + hf
                    for n in ("kh", "km", "kl"):
                        sp.wait_ge(S[n], c + 1)
                    sp.dma_start(k_dram[k, :, :, 2 * hf * HT:2 * (hf + 1) * HT].rearrange("s p t -> p s t"), k_part[:])\
                      .then_inc(S["k_out"], 16)
                    for n in ("qh", "qm", "ql"):
                        sp.wait_ge(S[n], c + 1)
                    sp.dma_start(q_dram[k, :, :, hf * HT:(hf + 1) * HT].rearrange("s p t -> p s t"), q_part[:])\
                      .then_inc(S["q_out"], 16)
                elif what == "stack":
                    sp.wait_ge(S["k_out"], 32 * (k + 1))
                    for m in range(2):
                        n = 2 * k + m
                        if n >= 3:
                            sp.wait_ge(S["scored"], 2 * NM * (n - 2))
                        for hpar in range(2):
                            rows = slice(64 * m + 32 * hpar, 64 * m + 32 * hpar + 32)
                            for s, n_slot, part in RUNS_K:
                                r = (hpar * NS + s) * DK
                                src = k_dram[k, part:part + n_slot, rows]
                                sp.dma_start(k_st[n % 3][r:r + n_slot * DK, :, :],
                                             src.rearrange("s (d q) t -> s d q t", q=4)).then_inc(k_in[n % 3], 16)
                        if m == 0:
                            sp.wait_ge(S["q_out"], 32 * (k + 1))
                        for hpar in range(2):
                            rows = slice(64 * m + 32 * hpar, 64 * m + 32 * hpar + 32)
                            for s, n_slot, part in RUNS_Q:
                                r = (hpar * NS + s) * DK
                                src = q_dram[k, part:part + 1, rows].broadcast_to([n_slot, 32, GT])
                                sp.dma_start(q_st[n % 3][r:r + n_slot * DK, :, :],
                                             src.rearrange("s (d q) t -> s d q t", q=4)).then_inc(q_in[n % 3], 16)
                    if k == 0:
                        for dst, src in ((wo[:], w_o), (wg[:], Wg), (bg_row[:], bg.partition_broadcast(128)),
                                         (w1[:], W1.rearrange("e d i -> d e i")),
                                         (w2[:], W2.rearrange("e i d -> i e d"))):
                            sp.dma_start(dst, src).then_inc(S["late_consts"], 16)
                elif what == "load_x1":
                    c = 2 * k + item[2]
                    if c:
                        sp.wait_ge(S["x1"], c)
                    if c >= 2:
                        sp.wait_ge(stored[item[2]], 16 * k)
                    sp.dma_start(x1[:, item[2], :, :], x_t[c]).then_inc(S["x_res"], 16)
                elif what == "out":
                    hf = item[2]
                    sp.wait_ge(S["y_out"], 2 * k + hf + 1)
                    sp.dma_start(o_t[2 * k + hf], x1[:, hf, :, :]).then_inc(stored[hf], 16)
            for hf in range(2):
                sp.wait_ge(stored[hf], 16 * G)

        @block.gpsimd
        def _(pool):
            pool.memset(mhalf[:], -0.5).then_inc(S["mhalf"], 1)

            def inverse_root(c, stat, variance, scaled, root, suffix):
                pool.wait_ge(S["mv" + suffix], TT * (c + 1))
                if c:
                    pool.wait_ge(S["rstd" + suffix], c)
                    pool.wait_ge(S["xn" + suffix], TT * c)
                pool.tensor_scalar(scaled[:], variance, EPS, None, ALU.add).then_inc(S["vare" + suffix], 1)
                pool.wait_ge(S["vare" + suffix], c + 1)
                if c == 0:
                    pool.wait_ge(S["mhalf"], 1)
                pool.tensor_tensor(root[:], scaled[:], mhalf[:], ALU.pow).then_inc(S["rstd" + suffix], 1)

            for item in steps:
                what, k = item[0], item[1]
                c = 2 * k + item[2] if len(item) > 2 else None
                if what == "stats1":
                    inverse_root(c, stats, mv[:, :, 1], vare, rstd, "")
                elif what == "stats2":
                    inverse_root(c, stats2, mv2[:, :, 1], vare2, rstd2, "2")
                elif what == "split":
                    what = item[3]
                    rest, part = parts_of[what]
                    pool.wait_ge(S[what + "m"], c + 1)
                    if c:
                        pool.wait_ge(S[what + "_out"], 16 * c)
                    pool.tensor_tensor(part[:, 2, :], rest, part[:, 1, :], ALU.subtract).then_inc(S[what + "l"], 1)
                elif what == "rows":
                    expand(pool, k, 1, S["shift_xp"])
                elif what == "pick" and item[4] % 2:
                    kind, e = item[3:]
                    n = (E // 2) * (2 * c + (kind == "down")) + e // 2
                    pick(pool, S["picked_p"], kind, c, e, n)


        @block.scalar
        def _(act):
            for item in steps:
                what, k = item[0], item[1]
                if what == "shift":
                    u = k
                    act.wait_ge(S["shifted"], u + 1)
                    v, ih = divmod(u, 2)
                    if v >= 2:
                        act.wait_ge(S["pv"], v - 1)
                    for h2 in range(2):
                        act.activation(prob[:, v % 2, h2 * GB:(h2 + 1) * GB, ih * IH:(ih + 1) * IH],
                                       score[u % 2][h2].rearrange("p (b i) -> p b i", i=IH), ACT.Exp, scale=SCALE)\
                           .then_inc(S["prob"], 1)
                    continue
                if what == "pv":
                    if item[2] != 3:
                        continue
                    act.wait_ge(S["pv"], k + 1)
                    g, m = divmod(k, NM)
                    if m == 0 and g:
                        act.wait_ge(S["attn_n"], 4 * g)
                    act.activation(att[:, :, 2 * m:2 * m + 2, :].rearrange("p n h v -> p n (h v)"),
                                   pv_ps.rearrange("p (n v) -> p n v", v=4 * VW), ACT.Copy)\
                       .then_inc(S["att"], 1)
                    continue
                if len(item) < 3 or what in ("load", "load_x1", "parts"):
                    continue
                hf = item[2]
                c = 2 * k + hf
                if what in ("xT", "cT"):
                    bank, done = read_wait(act, item)
                    if c:
                        act.wait_ge(S["q_done" if what == "xT" else "cT_used"], c)
                    if what == "xT":
                        act.activation(xT[:], bank, ACT.Copy).then_inc(S[what], 1)
                    else:
                        act.activation(cT[:], bank.unsqueeze(2).broadcast_to([128, HT, 2]), ACT.Copy)\
                           .then_inc(S[what], 1)
                    act.wait_ge(S[what], c + 1)
                    act.sem_inc(done, 1)
                elif what in ("q", "k"):
                    bank, done = read_wait(act, item)
                    full_f, part = parts_of[what]
                    if c:
                        act.wait_ge(S[what + "l"], c)
                    if what == "q":
                        if c == 0:
                            act.wait_ge(S["b_perm"], 1)
                        act.activation(full_f, bank, ACT.Identity, bias=b_perm[:, 0:1]).then_inc(S["qf"], 1)
                    else:
                        if c == 0:
                            act.wait_ge(S["consts"], 16 * N_CONST)
                        for x in range(2):
                            act.activation(kf[:, :, x], bank, ACT.Copy, scale=row_of[:, x:x + 1]).then_inc(S["kf"], 1)
                    n = (c + 1) * (1 if what == "q" else 2)
                    act.wait_ge(S[what + "f"], n)
                    act.sem_inc(done, 1)
                    if c:
                        act.wait_ge(S[what + "_out"], 16 * c)
                    act.activation(part[:, 0, :], full_f, ACT.Copy).then_inc(S[what + "h"], 1)
                elif what == "v" :
                    bank, done = read_wait(act, item)
                    if k >= 2:
                        act.wait_ge(S["pv"], NM * (k - 1))
                    b0 = hf * GB // 2 + item[3] * TT
                    for hpar in range(2):
                        src = bank.rearrange("p (b hpar h d) -> p b hpar h d", b=TT, hpar=2, d=DK)[:, :, hpar, :, :]
                        act.activation(val[k % 2][:, b0:b0 + TT, :, hpar * VW:hpar * VW + DK], src, ACT.Copy,
                                       scale=parity[:, hpar:hpar + 1]).then_inc(S["v_in"], 1)
                    act.wait_ge(S["v_in"], 4 * c + 2 * item[3] + 2)
                    act.sem_inc(done, 1)
                elif what == "aT":
                    bank, done = read_wait(act, item)
                    if c:
                        act.wait_ge(S["proj_done"], c)
                    act.activation(aT[:], bank, ACT.Copy).then_inc(S["aT"], 1)
                    act.wait_ge(S["aT"], c + 1)
                    act.sem_inc(done, 1)
                elif what == "x2T":
                    bank, done = read_wait(act, item)
                    if c:
                        act.wait_ge(S["gated"], c)
                        act.wait_ge(S["picked_v"], E * (c - 1) + E // 2)
                        act.wait_ge(S["picked_p"], E * (c - 1) + E // 2)
                    act.activation(x2T[:], bank, ACT.Copy).then_inc(S["x2T"], 1)
                    act.wait_ge(S["x2T"], c + 1)
                    act.sem_inc(done, 1)
                elif what == "ohT":
                    bank, done = read_wait(act, item)
                    if c:
                        act.wait_ge(S["oh_out"], 16 * c)
                    if c >= 2:
                        act.wait_ge(S["ffn_full"], 2 * (c - 1))
                    act.activation(ohT[:, hf, :], bank[0:3 * E, :], ACT.Copy).then_inc(S["ohT"], 1)
                    act.wait_ge(S["ohT"], c + 1)
                    act.sem_inc(done, 1)
                    act.dma_start(o_dram[c], ohT[0:E, hf, :]).then_inc(S["oh_out"], 16)
                elif what == "spread":
                    part = item[3]
                    act.wait_ge(S["oh_out"], 16 * (c + 1))
                    if c:
                        for n in ("picked_v", "picked_p"):
                            act.wait_ge(S[n], E * c - (0 if part else E // 4))
                    e = slice(part * E // 2, (part + 1) * E // 2)
                    act.dma_start(chosen[:, e, :], o_dram[c, e, :].partition_broadcast(128)).then_inc(chosen_in[part], 16)
                elif what == "gelu":
                    act.wait_ge(S["ffn_full"], 2 * c + 1)
                    if c:
                        act.wait_ge(S["picked_v"], E * c)
                        act.wait_ge(S["picked_p"], E * c)
                    act.activation(hid[:], ffn_ps, ACT.Gelu).then_inc(S["hid"], 1)
                elif what == "y":
                    act.wait_ge(S["ffn_full"], 2 * c + 2)
                    if c:
                        act.wait_ge(S["yT_used"], c)
                    act.activation(yT[:], ffn_ps, ACT.Copy).then_inc(S["yT"], 1)

        @block.vector
        def _(dve):
            dve.wait_ge(S["first_consts"], 16 * 4)

            def permute(dst, src):
                for hpar in range(2):
                    for mh in range(2):
                        o = dst[:, 64 * mh + 32 * hpar:64 * mh + 32 * hpar + 32]
                        i = src[:, 64 * hpar + 32 * mh:64 * hpar + 32 * mh + 32]
                        dve.tensor_copy(o.rearrange("k (d h2 ml) -> k ml h2 d", h2=2, ml=2),
                                        i.rearrange("k (ml h2 d) -> k ml h2 d", h2=2, ml=2)).then_inc(S["w_perm"], 1)

            permute(wq, wq_in)
            permute(wk, wk_in)

            def setup():
                dve.wait_ge(S["consts"], 16 * N_CONST)
                permute(wp, wp_in)
                dve.wait_ge(S["b_ps"], 1)
                dve.tensor_copy(b_perm[:], score[0][0][:, 0:2]).then_inc(S["b_perm"], 1)
                dve.tensor_copy(ident_h[:], ident[:]).then_inc(S["prep"], 1)
                dve.tensor_copy(shift_sel[:], shift_f).then_inc(S["prep"], 1)
                dve.tensor_copy(mask_f[:], mask_u[:]).then_inc(S["prep"], 1)
                dve.wait_ge(S["b_perm"], 1)
                dve.tensor_tensor(bias_diff[:], b_perm[:, 1:2], b_perm[:, 0:1], ALU.subtract).then_inc(S["prep"], 1)
                dve.wait_ge(S["prep"], 4)
                dve.tensor_scalar(bias_heads[:], head_of, bias_diff[:, 0:1], None, ALU.mult)\
                   .then_inc(S["bias_heads"], 1)
                for hpar in range(2):
                    dve.tensor_scalar(mask_neg[:, :, hpar], mask_f[0:64, :], 1.0, NEG, ALU.subtract, ALU.mult)\
                       .then_inc(S["prep"], 1)
                dve.tensor_reduce(any_key[:, 0:1], mask_f[:], AX, ALU.max).then_inc(S["prep"], 1)
                dve.wait_ge(S["prep"], 7)
                dve.reciprocal(any_key[:, 1:2], any_key[:, 0:1]).then_inc(S["prep"], 1)
                dve.wait_ge(S["prep"], 8)
                dve.tensor_tensor(any_key[:, 2:3], any_key[:, 0:1], any_key[:, 1:2], ALU.mult).then_inc(S["prep"], 1)
                dve.wait_ge(S["ph_rev"], 1)
                for x in range(2):
                    dve.tensor_scalar(rev[:, 0, :].rearrange("p (t x) -> p t x", x=2)[:, :, x], score[0][1][:, 0:128],
                                      row_of[:, x:x + 1], None, ALU.mult).then_inc(S["rev"], 1)
                dve.wait_ge(S["rev"], 2)
                split(rev[:, 0, :], rev[:, 1, :], [rev_part[:, s, :] for s in range(3)], S["rev_split"], 0)
                dve.wait_ge(S["ph_cst"], 1)
                dve.tensor_copy(cst[:, 0, :], score[1][0][0:H, 0:256]).then_inc(S["rev"], 1)
                dve.wait_ge(S["rev"], 3)
                split(cst[:, 0, :], cst[:, 1, :], [cst_part[:, s, :] for s in range(3)], S["cst_split"], 0)
                for i in range(2):
                    for hpar in range(2):
                        dve.tensor_copy(val[i][:, :, :, hpar * VW + DK],
                                        parity[:, hpar:hpar + 1].unsqueeze(2).broadcast_to([128, GB, HP]))\
                           .then_inc(S["val_ones"], 1)
                split(b12[:], b12_rest[:], [b12_part[:, :, s, :] for s in range(3)], S["bias_split"], 0)

            def split(whole, rest, parts, done, n):
                dve.tensor_copy(parts[0], whole).then_inc(done, 1)
                dve.wait_ge(done, n + 1)
                dve.tensor_tensor(rest, whole, parts[0], ALU.subtract).then_inc(done, 1)
                dve.wait_ge(done, n + 2)
                dve.tensor_copy(parts[1], rest).then_inc(done, 1)
                dve.wait_ge(done, n + 3)
                dve.tensor_tensor(parts[2], rest, parts[1], ALU.subtract).then_inc(done, 1)

            def norm_stats(c, tiles, stat, agg, suffix):
                if c:
                    dve.wait_ge(S["xn" + suffix], TT * c)
                    dve.wait_ge(S["rstd" + suffix], c)
                for t in range(TT):
                    dve.bn_stats(stat[:, t, :], tiles(t)).then_inc(S["stats" + suffix], 1)
                for t in range(TT):
                    dve.wait_ge(S["stats" + suffix], TT * c + t + 1)
                    dve.bn_aggr(agg[:, t, :], stat[:, t, :]).then_inc(S["mv" + suffix], 1)

            def norm_apply(c, tiles, agg, root, dst, suffix):
                dve.wait_ge(S["rstd" + suffix], c + 1)
                dve.wait_ge(S["mv" + suffix], TT * (c + 1))
                for t in range(TT):
                    dve.tensor_scalar(dst[:, t, :], tiles(t), agg[:, t, 0:1], root[:, t:t + 1],
                                      ALU.subtract, ALU.mult).then_inc(S["xn" + suffix], 1)

            for item in steps:
                what, k = item[0], item[1]
                if what == "setup":
                    setup()
                    continue
                if what == "scores":
                    u = k
                    if u >= 2:
                        dve.wait_ge(S["rows"], u - 1)
                    h2 = item[2]
                    n = 2 * u + h2
                    dve.wait_ge(S["scored"], n + 1)
                    if n:
                        dve.wait_ge(S["colmaxed"], n)
                    dve.transpose(turned[:], score[u % 2][h2]).then_inc(S["turned"], 1)
                    dve.wait_ge(S["turned"], n + 1)
                    dve.tensor_reduce(colmax[:, u % 2, h2, :, :], turned[:].rearrange("p (b j x) -> p b x j", b=GB, x=2),
                                      AX, ALU.max).then_inc(S["colmaxed"], 1)
                    continue
                if what == "rows":
                    u = k
                    dve.wait_ge(S["rows"], u + 1)
                    if u:
                        dve.wait_ge(S["shift_v"], u)
                    dve.tensor_reduce(rowmax[:], row_ps.rearrange("p (jh i) -> p i jh", jh=4), AX, ALU.max)\
                       .then_inc(S["rowmaxed"], 1)
                    dve.wait_ge(S["rowmaxed"], u + 1)
                    dve.tensor_copy(rowmax_h[:], rowmax[:]).then_inc(S["rowmax_h"], 1)
                    dve.wait_ge(S["rowmax_h"], u + 1)
                    if u >= 2:
                        dve.wait_ge(S["shift_xv"], u - 1)
                        dve.wait_ge(S["shift_xp"], u - 1)
                    dve.scalar_tensor_tensor(shift_v[:, u % 2, :], rowmax_h[:], minus_lo, rowmax[:],
                                             ALU.mult, ALU.add).then_inc(S["shift_v"], 1)
                    expand(dve, u, 0, S["shift_xv"])
                    continue
                if len(item) < 3 or what in ("load", "load_x1", "parts"):
                    continue
                hf = item[2]
                c = 2 * k + hf
                if what == "stats1":
                    dve.wait_ge(S["x_in"], 16 * (c + 1))
                    norm_stats(c, lambda t: x_in[:, t, :], stats, mv, "")
                elif what == "ln1":
                    norm_apply(c, lambda t: x_in[:, t, :], mv, rstd, x_in, "")
                elif what == "split":
                    what = item[3]
                    full_f, part = parts_of[what]
                    dve.wait_ge(S[what + "h"], c + 1)
                    dve.wait_ge(S[what + "f"], (c + 1) * (1 if what == "q" else 2))
                    dve.tensor_tensor(full_f, full_f, part[:, 0, :], ALU.subtract).then_inc(S["r1" + what], 1)
                    dve.wait_ge(S["r1" + what], c + 1)
                    if c:
                        dve.wait_ge(S[what + "_out"], 16 * c)
                    dve.tensor_copy(part[:, 1, :], full_f).then_inc(S[what + "m"], 1)
                elif what == "norm":
                    dve.wait_ge(S["att"], NM * (k + 1))
                    sums = att[:, hf * TT:(hf + 1) * TT, :, :].rearrange("p n h (hpar v) -> p (n h hpar) v", hpar=2)
                    if c:
                        dve.wait_ge(S["attn_n"], 2 * c)
                    dve.reciprocal(rden[:], sums[:, :, DK]).then_inc(S["rden"], 1)
                    dve.wait_ge(S["rden"], c + 1)
                    if c >= 2:
                        dve.wait_ge(S["aT_used"], c - 1)
                    for hpar in range(2):
                        dve.scalar_tensor_tensor(
                            att_n[:, hf, :, :].rearrange("p n (hpar h d) -> p n hpar h d", hpar=2, d=DK)[:, :, hpar, :, :],
                            att[:, hf * TT:(hf + 1) * TT, :, hpar * VW:hpar * VW + DK], any_key[:, 2:3],
                            rden[:].rearrange("p (n h hpar) -> p n h hpar", n=TT, hpar=2)[:, :, :, hpar]
                            .unsqueeze(3).broadcast_to([128, TT, HP, DK]), ALU.mult, ALU.mult)\
                           .then_inc(S["attn_n"], 1)
                elif what == "proj":
                    bank, done = read_wait(dve, item)
                    dve.wait_ge(S["x_res"], 16 * (c + 1))
                    dve.tensor_tensor(x1[:, hf, :, :], bank.rearrange("p (n d) -> p n d", d=D),
                                      x1[:, hf, :, :], ALU.add).then_inc(S["x1"], 1)
                    dve.wait_ge(S["x1"], c + 1)
                    dve.sem_inc(done, 1)
                elif what == "stats2":
                    norm_stats(c, lambda t: x1[:, hf, t, :], stats2, mv2, "2")
                elif what == "ln2":
                    if c:
                        dve.wait_ge(S["x2T"], c)
                    norm_apply(c, lambda t: x1[:, hf, t, :], mv2, rstd2, xn2, "2")
                elif what == "gate":
                    bank, done = read_wait(dve, item)
                    if c:
                        dve.wait_ge(S["onehot"], c)
                    else:
                        dve.wait_ge(S["late_consts"], 16 * 5)
                    dve.tensor_tensor(logit[:], bank[:, 0:TT * E].rearrange("p (n e) -> p n e", e=E),
                                      bg_row[:].unsqueeze(1).broadcast_to([128, TT, E]), ALU.add)\
                       .then_inc(S["logit"], 1)
                    dve.wait_ge(S["logit"], c + 1)
                    dve.sem_inc(done, 1)
                    dve.tensor_reduce(top[:], logit[:], AX, ALU.max).then_inc(S["top"], 1)
                    dve.wait_ge(S["top"], c + 1)
                    dve.tensor_tensor(is_top[:], logit[:], top[:].unsqueeze(2).broadcast_to([128, TT, E]),
                                      ALU.is_equal).then_inc(S["is_top"], 1)
                    dve.wait_ge(S["is_top"], c + 1)
                    dve.tensor_tensor(key[:], is_top[:], order.unsqueeze(1).broadcast_to([128, TT, E]),
                                      ALU.mult).then_inc(S["key"], 1)
                    dve.wait_ge(S["key"], c + 1)
                    dve.tensor_reduce(first[:], key[:], AX, ALU.max).then_inc(S["first"], 1)
                    dve.wait_ge(S["first"], c + 1)
                    if c:
                        dve.wait_ge(S["ohT"], c)
                    for s in range(3):
                        last = dve.tensor_tensor(onehot[:, :, s, :], key[:],
                                                 first[:].unsqueeze(2).broadcast_to([128, TT, E]), ALU.is_equal)
                    last.then_inc(S["onehot"], 1)
                elif what == "pick" and item[4] % 2 == 0:
                    kind, e = item[3:]
                    pick(dve, S["picked_v"], kind, c, e, (E // 2) * (2 * c + (kind == "down")) + e // 2)
                elif what == "out":
                    bank, done = read_wait(dve, item)
                    dve.tensor_tensor(x1[:, hf, :, :], bank.rearrange("p (n d) -> p n d", d=D), x1[:, hf, :, :], ALU.add)\
                       .then_inc(S["y_out"], 1)
                    dve.wait_ge(S["y_out"], c + 1)
                    dve.sem_inc(done, 1)

        @block.tensor
        def _(pe):
            def setup():
                pe.wait_ge(S["consts"], 16 * N_CONST)
                pe.matmul(score[0][0][:, 0:2], perm, b_uv[:], start=True, stop=True).then_inc(S["b_ps"], 1)
                pe.wait_ge(S["w_perm"], 12)
                pe.matmul(score[0][1][:, 0:128], wp, pe_rev, start=True, stop=True).then_inc(S["ph_rev"], 1)
                pe.wait_ge(S["bias_heads"], 1)
                pe.wait_ge(S["rev"], 2)
                pe.matmul(score[1][0][0:H, 0:256], bias_heads[:], rev[:, 0, :], start=True, stop=True)\
                  .then_inc(S["ph_cst"], 1)

            def transposes(item, tiles, rows=128):
                bank, done = fill_wait(pe, item)
                for t in range(TT):
                    last = pe.transpose(bank[0:rows, t * 128:(t + 1) * 128], tiles(t), ident[:])
                return last, done

            def pv(v, part):
                g, m = divmod(v, NM)
                if part == 0:
                    pe.wait_ge(S["prob"], 4 * (v + 1))
                pe.wait_ge(S["v_in"], 8 * (g + 1))
                if v == 0:
                    pe.wait_ge(S["val_ones"], 4)
                pe.wait_ge(S["rowmaxed"], min(2 * v + 3, NU))
                if v:
                    pe.wait_ge(S["att"], v)
                for b in range(part * GB // 4, (part + 1) * GB // 4):
                    r = 64 * (b % 2)
                    for h2 in range(2):
                        at = ((b // 2) * 2 + h2) * 2 * VW
                        last = pe.matmul(pv_ps[r:r + 64, at:at + 2 * VW], prob[:, v % 2, h2 * GB + b, :],
                                         val[g % 2][:, b, 2 * m + h2, :], start=True, stop=True)
                if part == 3:
                    last.then_inc(S["pv"], 1)

            for item in steps:
                what, k = item[0], item[1]
                if what == "setup":
                    setup()
                elif what == "scores":
                    u = k
                    v, ih = divmod(u, 2)
                    n, ml = divmod(v, NM // 2)
                    m = v % NM
                    if ih == 0 and ml == 0 and item[2] == 0:
                        pe.wait_ge(q_in[n % 3], 16 * 6 * (n // 3 + 1))
                        pe.wait_ge(k_in[n % 3], 16 * 6 * (n // 3 + 1))
                    if u == 0 and item[2] == 0:
                        pe.wait_ge(S["prep"], 7)
                        pe.wait_ge(S["rev"], 3)
                        pe.wait_ge(S["pos_in"], 16 * 13)
                        pe.wait_ge(S["ones"], 16 * 3)
                    if u >= 2:
                        pe.wait_ge(S["prob"], 2 * (u - 2) + item[2] + 1)
                    qs, ks = q_st[n % 3], k_st[n % 3]
                    h2, i0 = item[2], ih * IH
                    bank = score[u % 2][h2]
                    keys = ks[0:KC, 2 * h2 + ml, :]
                    query = qs[0:KB, 2 * h2 + ml, :].rearrange("p (b t) -> p b t", b=GB)
                    at = bank.rearrange("p (b i) -> p b i", b=GB)
                    for b in range(GB):
                        pe.matmul(at[:, b, :], keys[:, b * 2 * T:(b + 1) * 2 * T], query[0:KC, b, i0:i0 + IH],
                                  start=(b == 0), stop=False, skip_group_check=True)
                    for i in range(IH):
                        t = 2 * (T - 1 - i0 - i)
                        pe.matmul(at[:, :, i], pos[0:KB, 4 * (m // 2) + 2 * h2 + ml, t:t + 2 * T],
                                  query[:, :, i0 + i], start=False, stop=False, skip_group_check=True)
                    pe.matmul(bank, mask_neg[:].rearrange("p j x -> p (j x)"),
                              ident_h[0:64, i0:i0 + IH].unsqueeze(1).broadcast_to([64, GB, IH]),
                              start=False, stop=True, skip_group_check=True).then_inc(S["scored"], 1)
                elif what == "rows":
                    u = k
                    pe.wait_ge(S["colmaxed"], 2 * (u + 1))
                    if u >= 3:
                        pe.wait_ge(S["att"], (u - 1) // 2)
                    for part in range(2):
                        last = pe.matmul(row_ps[64 * part:64 * part + 64, :],
                                         colmax[:, u % 2, :, :, :].rearrange("p h b x -> p (h b x)"), ident[:],
                                         start=True, stop=True)
                    last.then_inc(S["rows"], 1)
                elif what == "pv":
                    pv(k, item[2])
                elif what == "shift":
                    u = k
                    for h2 in range(2):
                        pe.wait_ge(S["shift_xp" if h2 else "shift_xv"], u + 1)
                        last = pe.matmul(score[u % 2][h2], shift_sel[:], shift_x[:, u % 2, h2, :, :], start=False,
                                         stop=True, skip_group_check=True)
                    last.then_inc(S["shifted"], 1)
                elif what in ("load", "load_x1", "stack", "stats1", "ln1", "stats2", "ln2", "split", "norm", "parts", "tables", "spread",
                              "pick"):
                    pass
                else:
                    hf = item[2]
                    c = 2 * k + hf
                    if what == "xT":
                        pe.wait_ge(S["xn"], TT * (c + 1))
                        if c == 0:
                            pe.wait_ge(S["first_consts"], 16 * 4)
                        last, done = transposes(item, lambda t: x_in[:, t, :])
                        last.then_inc(done, 1)
                        pe.wait_ge(done, turn[item] // 2 + 1)
                        pe.sem_inc(S["xT_used"], 1)
                    elif what == "cT":
                        pe.wait_ge(S["c_in"], 16 * (c + 1))
                        last, done = transposes(item, lambda t: c_in[:, t, :])
                        last.then_inc(done, 1)
                    elif what == "q":
                        bank, done = fill_wait(pe, item)
                        pe.wait_ge(S["xT"], c + 1)
                        if c == 0:
                            pe.wait_ge(S["w_perm"], 8)
                        pe.matmul(bank, wq[:], xT[:], start=True, stop=True).then_inc(done, 1)
                        pe.wait_ge(done, turn[item] // 2 + 1)
                        pe.sem_inc(S["q_done"], 1)
                    elif what == "k":
                        bank, done = fill_wait(pe, item)
                        pe.wait_ge(S["cT"], c + 1)
                        pe.matmul(bank, wk[:], cT[:, :, 0], start=True, stop=True).then_inc(done, 1)
                    elif what == "v":
                        bank, done = fill_wait(pe, item)
                        both = cT[:].rearrange("p j x -> p (j x)")
                        for n in range(TT):
                            b = item[3] * TT + n
                            last = pe.matmul(bank[:, n * 128:(n + 1) * 128], both[:, b * 2 * T:(b + 1) * 2 * T], wv[:],
                                             start=True, stop=True)
                        last.then_inc(done, 1)
                        if item[3]:
                            pe.wait_ge(done, turn[item] // 2 + 1)
                            pe.sem_inc(S["cT_used"], 1)
                    elif what == "aT":
                        pe.wait_ge(S["attn_n"], 2 * (c + 1))
                        last, done = transposes(item, lambda t: att_n[:, hf, t, :])
                        last.then_inc(done, 1)
                        pe.wait_ge(done, turn[item] // 2 + 1)
                        pe.sem_inc(S["aT_used"], 1)
                    elif what == "proj":
                        bank, done = fill_wait(pe, item)
                        pe.wait_ge(S["aT"], c + 1)
                        if c == 0:
                            pe.wait_ge(S["late_consts"], 16 * 5)
                        for t in range(TT):
                            last = pe.matmul(bank[:, t * 128:(t + 1) * 128], aT[:, t * 128:(t + 1) * 128], wo[:],
                                             start=True, stop=True)
                        last.then_inc(done, 1)
                        pe.wait_ge(done, turn[item] // 2 + 1)
                        pe.sem_inc(S["proj_done"], 1)
                    elif what == "x2T":
                        pe.wait_ge(S["xn2"], TT * (c + 1))
                        last, done = transposes(item, lambda t: xn2[:, t, :])
                        last.then_inc(done, 1)
                    elif what == "gate":
                        bank, done = fill_wait(pe, item)
                        pe.wait_ge(S["x2T"], c + 1)
                        for t in range(TT):
                            last = pe.matmul(bank[:, t * E:(t + 1) * E], x2T[:, t * 128:(t + 1) * 128], wg[:],
                                             start=True, stop=True)
                        last.then_inc(done, 1)
                        pe.wait_ge(done, turn[item] // 2 + 1)
                        pe.sem_inc(S["gated"], 1)
                    elif what == "ohT":
                        pe.wait_ge(S["onehot"], c + 1)
                        last, done = transposes(item, lambda t: onehot[:, t, :, :].rearrange("p s e -> p (s e)"), 3 * E)
                        last.then_inc(done, 1)
                    elif what in ("up", "down"):
                        e = item[3]
                        n = (E // 2) * (2 * c + (what == "down")) + e // 2
                        pe.wait_ge(S["picked_p" if e % 2 else "picked_v"], n + 1)
                        if e == 0:
                            if what == "down":
                                pe.wait_ge(S["hid"], c + 1)
                            elif c:
                                pe.wait_ge(S["yT"], c)
                        pe.matmul(ffn_ps, (w1 if what == "up" else w2)[:, e, :], picked[:, 2 * (e % 2) + n % 2, :],
                                  start=(e == 0), stop=False).then_inc(S[what], 1)
                    elif what in ("gelu", "y"):
                        if c == 0 and what == "gelu":
                            pe.wait_ge(S["bias_in"], 48)
                        pe.matmul(ffn_ps, b12_rows[:, 0 if what == "gelu" else 1, :], ohT[:, hf, :], start=False, stop=True)\
                          .then_inc(S["ffn_full"], 1)
                    elif what == "out":
                        pe.wait_ge(S["yT"], c + 1)
                        last, done = transposes(item, lambda t: yT[:, t * 128:(t + 1) * 128])
                        last.then_inc(done, 1)
                        pe.wait_ge(done, turn[item] // 2 + 1)
                        pe.sem_inc(S["yT_used"], 1)


def constants():
    import numpy as np
    ident = np.eye(128, dtype=np.float32)
    theta = np.arange(T, dtype=np.float32)[:, None] / np.float32(10000.0) ** (
        np.arange(0, D, 2, dtype=np.float32) / np.float32(D))
    enc = np.stack([np.sin(theta), np.cos(theta)], axis=-1).reshape(T, D)
    pe = np.zeros((D, 128), np.float32)
    pe[:, 0:T] = enc[::-1].T
    small = np.zeros((128, 64), np.float32)
    p = np.arange(128)
    mh, hpar, d, h2, ml = p // 64, p // 32 % 2, p // 4 % 8, p // 2 % 2, p % 2
    perm = np.zeros((128, 128), np.float32)
    perm[((hpar * 2 + mh) * 2 + ml) * 16 + h2 * 8 + d, p] = 1.0
    small[p, hpar * 8 + mh * 4 + h2 * 2 + ml] = 1.0
    small[p, 57 + hpar] = 1.0
    small[p, 59 + p % 2] = 1.0
    small[:, 16] = -1.0 * (p // 64 == 1)
    small[p, 17 + p // 2 % 32] = 1.0
    small[:, 49:57] = E - np.arange(E)
    shift = np.where((p % 2)[:, None] == (p % 2)[None, :], -1.0, 0.0).astype(np.float32)
    ones = np.full((6, HP // 2, GT), 0x3F80, np.uint16)
    return {"c_ident": ident, "c_pe": pe, "c_small": small, "c_shift": shift, "c_perm": perm, "c_ones": ones}


_INS = ["x", "ctx_1024", "mask_1xSxS2_bf1", "L0_xattn_w_q", "L0_xattn_w_k", "L0_xattn_w_v", "L0_xattn_w_p",
        "L0_xattn_w_o", "L0_xattn_b_u", "L0_xattn_b_v", "L0_ffn_Wg", "L0_ffn_bg", "L0_ffn_W1", "L0_ffn_b1",
        "L0_ffn_W2", "L0_ffn_b2"]


def kernel(**inputs):
    import numpy as _np
    import concourse.bacc as _bacc
    from concourse import mybir as _mybir
    from concourse.bass_utils import run_bass_kernel_spmd as _run

    nc = _bacc.Bacc("TRN2", target_bir_lowering=False, num_devices=1)
    arrays, args = {}, []

    def give(name, a):
        arrays[name] = a
        args.append(nc.dram_tensor(name, a.shape, _mybir.dt.from_np(a.dtype), kind="ExternalInput").ap())

    for name in _INS:
        a = _np.ascontiguousarray(inputs[name])
        give(f"in_{name}_dram", a.view(_np.uint8) if a.dtype == _np.bool_ else a)
    for name, a in constants().items():
        give(name, a)
    args.append(nc.dram_tensor("out_0_dram", (B, T, D), _mybir.dt.float32, kind="ExternalOutput").ap())
    xattn_moe_kernel(nc, *args)
    r = _run(nc, [arrays], core_ids=[0])
    return r.results[0]["out_0_dram"]
```
